# Optimizing a Trainium2 kernel written in Bass

```python
import numpy as np
import jax
import jax.numpy as jnp

def _softmax(x, axis=-1):
    return jax.nn.softmax(x, axis=axis)

def _gelu(x):
    return jax.nn.gelu(x, approximate=True)

def _silu(x):
    return jax.nn.silu(x)

def _sigmoid(x):
    return jax.nn.sigmoid(x)

def _layernorm(x, axis=-1, eps=1e-05):
    m = jnp.mean(x, axis=axis, keepdims=True)
    v = jnp.var(x, axis=axis, keepdims=True)
    return (x - m) / jnp.sqrt(v + eps)

def _scatter_add(tgt, idx, src, axis=0):
    return tgt.at[idx].add(src)

def _segment_sum(src, seg, n):
    return jax.ops.segment_sum(src, seg, n)
kernel_name = 'mk_cond_resid_d2_seqx_r2_d013e9'

def setup_inputs(seed: int=0):
    np.random.seed(seed)
    _w = jnp.asarray

    def _rec_inputs():
        import jax
        import jax.numpy as jnp
        _rk = jax.random.key(seed)
        x = -0.0003929 + 0.9999 * jax.random.normal(jax.random.fold_in(_rk, 1), (8, 512, 512), jnp.float32)
        _lenS = 512 - jax.random.randint(jax.random.fold_in(_rk, 7), (8,), 0, max(1, 512 // 4) + 1, jnp.int32)
        _lenS2 = 512 - jax.random.randint(jax.random.fold_in(_rk, 8), (8,), 0, max(1, 512 // 4) + 1, jnp.int32)
        cond_1024 = 0.00386106 + 1.00199 * jax.random.normal(jax.random.fold_in(_rk, 11), (8, 512), jnp.float32)
        return (x, cond_1024)
    x, cond_1024 = _rec_inputs()

    def _L0_cond_setup():
        import jax, jax.numpy as jnp
        import numpy as np
        RANK = 8
        LN_EPS = 1e-05
        key = jax.random.key(seed)
        ks = jax.random.split(key, 8)
        B, T, D = (16, 512, 512)
        A = 512
        I = 512
        OUT = D * RANK * 4
        s = 0.02
        return {'x': jax.random.normal(ks[0], (B, T, D), jnp.float32), 'ada_emb': jax.random.normal(ks[1], (B, A), jnp.float32), 'base_up': jax.random.normal(ks[2], (D, D), jnp.float32) * s, 'base_down': jax.random.normal(ks[3], (D, D), jnp.float32) * s, 'ln_gamma': jnp.ones((A,), jnp.float32), 'ln_beta': jnp.zeros((A,), jnp.float32), 'W1': jax.random.normal(ks[4], (A, I), jnp.float32) / np.sqrt(A), 'bias1': jnp.zeros((I,), jnp.float32), 'W2': jax.random.normal(ks[5], (I, OUT), jnp.float32) / np.sqrt(I), 'bias2': jnp.zeros((OUT,), jnp.float32)}
    _L0_cond_all = _L0_cond_setup()
    _L0_cond_in = {k: v for k, v in _L0_cond_all.items() if k in ('base_up', 'base_down', 'ln_gamma', 'ln_beta', 'W1', 'bias1', 'W2', 'bias2')}
    del _L0_cond_all

    def _L1_cond_setup():
        import jax, jax.numpy as jnp
        import numpy as np
        import math
        N, T, D, H = (64, 256, 512, 512)
        key = jax.random.key(seed)
        k1, k2, k3, k4 = jax.random.split(key, 4)
        x = jax.random.normal(k1, (N, T, D), dtype=jnp.float32)
        h0 = jax.random.normal(k2, (N, H), dtype=jnp.float32)
        Wx = jax.random.normal(k3, (D, 4 * H), dtype=jnp.float32) / math.sqrt(D)
        Wh = jax.random.normal(k4, (H, 4 * H), dtype=jnp.float32) / math.sqrt(H)
        b = jnp.zeros((4 * H,), dtype=jnp.float32)
        return {'x': x, 'h0': h0, 'Wx': Wx, 'Wh': Wh, 'b': b}
    _L1_cond_all = _L1_cond_setup()
    _L1_cond_in = {k: v for k, v in _L1_cond_all.items() if k in ('Wx', 'Wh', 'b')}
    del _L1_cond_all
    return {'x': x, 'cond_1024': cond_1024, 'L0_cond_base_up': _L0_cond_in['base_up'], 'L0_cond_base_down': _L0_cond_in['base_down'], 'L0_cond_ln_gamma': _L0_cond_in['ln_gamma'], 'L0_cond_ln_beta': _L0_cond_in['ln_beta'], 'L0_cond_W1': _L0_cond_in['W1'], 'L0_cond_bias1': _L0_cond_in['bias1'], 'L0_cond_W2': _L0_cond_in['W2'], 'L0_cond_bias2': _L0_cond_in['bias2'], 'L1_cond_Wx': _L1_cond_in['Wx'], 'L1_cond_Wh': _L1_cond_in['Wh'], 'L1_cond_b': _L1_cond_in['b']}

def reference(x, cond_1024, L0_cond_base_up, L0_cond_base_down, L0_cond_ln_gamma, L0_cond_ln_beta, L0_cond_W1, L0_cond_bias1, L0_cond_W2, L0_cond_bias2, L1_cond_Wx, L1_cond_Wh, L1_cond_b):
    import jax
    import jax.numpy as jnp

    def _L0_cond_ref(x, ada_emb, base_up, base_down, ln_gamma, ln_beta, W1, bias1, W2, bias2):
        import jax, jax.numpy as jnp
        import numpy as np
        RANK = 8
        LN_EPS = 1e-05
        B, T, D = x.shape
        R = RANK
        mu = jnp.mean(ada_emb, axis=-1, keepdims=True)
        var = jnp.mean(jnp.square(ada_emb - mu), axis=-1, keepdims=True)
        c = (ada_emb - mu) / jnp.sqrt(var + LN_EPS) * ln_gamma + ln_beta
        h = jax.nn.gelu(c @ W1 + bias1, approximate=False)
        w = h @ W2 + bias2
        a1, b1, a2, b2 = [t.reshape(B, D, R) for t in jnp.split(w, 4, axis=-1)]
        u = jnp.einsum('btd,bdr->btr', x, a2)
        mid = jnp.einsum('btd,dl->btl', x, base_down) + jnp.einsum('btr,blr->btl', u, b2)
        mid = jax.nn.gelu(mid, approximate=False)
        v = jnp.einsum('blr,btl->btr', b1, mid)
        out = jnp.einsum('btl,kl->btk', mid, base_up) + jnp.einsum('bkr,btr->btk', a1, v)
        return x + out

    def _L1_cond_ref(x, h0, Wx, Wh, b):
        import jax, jax.numpy as jnp
        import numpy as np
        import math
        N, T, D, H = (64, 256, 512, 512)
        Hdim = h0.shape[1]
        xW = jnp.einsum('ntd,dg->ntg', x, Wx) + b

        def step(carry, xw_t):
            prev_h, prev_c = carry
            a = xw_t + prev_h @ Wh
            i = jax.nn.sigmoid(a[:, :Hdim])
            f = jax.nn.sigmoid(a[:, Hdim:2 * Hdim])
            o = jax.nn.sigmoid(a[:, 2 * Hdim:3 * Hdim])
            g = jnp.tanh(a[:, 3 * Hdim:])
            next_c = f * prev_c + i * g
            next_h = o * jnp.tanh(next_c)
            return ((next_h, next_c), next_h)
        c0 = jnp.zeros_like(h0)
        _, hs = jax.lax.scan(step, (h0, c0), jnp.swapaxes(xW, 0, 1))
        return jnp.swapaxes(hs, 0, 1)
    x = x + _L0_cond_ref(x, cond_1024, L0_cond_base_up, L0_cond_base_down, L0_cond_ln_gamma, L0_cond_ln_beta, L0_cond_W1, L0_cond_bias1, L0_cond_W2, L0_cond_bias2)
    x = x + _L1_cond_ref(x, cond_1024, L1_cond_Wx, L1_cond_Wh, L1_cond_b)
    return x

_drawn_inputs = setup_inputs


def setup_inputs(seed=0):
    import zlib

    import numpy as np

    out = dict(_drawn_inputs(seed))
    spreads = {'L0_cond_ln_gamma': (1.0, 0.2),
     'L0_cond_ln_beta': (0.0, 0.1),
     'L0_cond_bias1': (0.0, 0.1),
     'L0_cond_bias2': (0.0, 0.1),
     'L1_cond_b': (0.0, 0.8)}
    factors = {'L0_cond_base_up': 3.721, 'L0_cond_base_down': 3.638, 'L1_cond_Wx': 8.0, 'L1_cond_Wh': 8.0}
    for name, (base, spread) in spreads.items():
        noise = np.random.default_rng([zlib.crc32(name.encode()), seed]).standard_normal(out[name].shape)
        drawn = base * np.exp(spread * noise) if base else spread * noise
        out[name] = jnp.asarray(drawn.astype(out[name].dtype))
    for name, factor in factors.items():
        out[name] = (out[name] * factor).astype(out[name].dtype)
    return out
```

```python
from contextlib import ExitStack

import concourse.bass as bass
from concourse import mybir

P = 128
F32 = mybir.dt.float32
BF16 = mybir.dt.bfloat16
ALU = mybir.AluOpType
ACT = mybir.ActivationFunctionType
AX = mybir.AxisListType

BT = 16
GATES = 4
PARTS = 3
GROUP = 32
SLOTS = 15
LN_EPS = 1e-5


def cond_residual_lstm(nc, x, cond, base_up, base_down, ln_gamma, ln_beta, w1, bias1, w2, bias2,
                       wx, wh, bias_g, ident_in, fold_in, mask_in, out):
    B, T, D = x.shape
    KC = D // P
    HC = KC // 2
    NB = T // BT
    R = w2.shape[1] // (4 * D)
    BR = B * R
    TOK = BT * B
    HG = HC * B
    FLAT = 2 * P
    assert TOK == P and D == 512 and NB % 2 == 0 and PARTS * B <= GROUP

    with ExitStack() as ctx:
        def sb(name, shape, dt=F32):
            return ctx.enter_context(nc.sbuf_tensor(name, shape, dt))

        def psum(name):
            return ctx.enter_context(nc.psum_tensor(name, [P, 512], F32))

        def sem(name):
            return ctx.enter_context(nc.semaphore(name))

        ident = sb("ident", [P, P])
        fold = sb("fold", [P, GATES * B])
        mask = sb("mask", [BR, TOK])
        wh_parts = sb("wh_parts", [P, PARTS, KC, GATES * D], BF16)
        wx_sb = sb("wx_sb", [P, KC, GATES * D])
        down_sb = sb("down_sb", [P, KC, D])
        up_t = sb("up_t", [P, KC, D])
        ada = sb("ada", [P, 4, KC, BR])
        a1_t = sb("a1_t", [BR, D])
        b2_t = sb("b2_t", [BR, D])

        w2_sb = [sb(f"w2_sb{i}", [P, KC, D * R // KC]) for i in range(KC)]
        bias2_sb = sb("bias2_sb", [P, 4, KC, R])
        cond_sb = sb("cond_sb", [B, D])
        cond_n = sb("cond_n", [B, D])
        cond_sq = sb("cond_sq", [B, D])
        stat = sb("stat", [B, 12])
        VECS = (3 + GATES) * KC
        vec_rows = sb("vec_rows", [VECS, P])
        vecs_t = sb("vecs_t", [P, VECS])
        gamma_t, beta_t, bias1_t = (vecs_t[:, KC * i:KC * i + KC] for i in range(3))
        gate_bias = vecs_t[:, 3 * KC:].rearrange("p (j h c) -> p h j c", j=GATES, h=2)
        cond_t = sb("cond_t", [P, KC, B])
        hid_t = sb("hid_t", [P, KC, B])

        x_sb = sb("x_sb", [TOK, D])
        x_t = sb("x_t", [P, KC, TOK])
        u_m = sb("u_m", [BR, TOK])
        v_m = sb("v_m", [BR, TOK])
        def later(i):
            return w2_sb[KC - 1][:].rearrange("p k c -> p (k c)")[:, i * D:i * D + D]

        mid_t = later(0).rearrange("p (c t) -> p c t", t=TOK)
        x1_t = [sb(f"x1_t{i}", [P, KC, TOK]) for i in range(2)]
        xw = [sb(f"xw{i}", [P, BT, 2, GATES * HG]) for i in range(2)]
        up_raw = xw[1][:].rearrange("p t h g -> p (t h g)").rearrange("p (k l) -> p k l", k=KC)
        w1_sb = xw[0][:].rearrange("p t h g -> p (t h g)").rearrange("p (k l) -> p k l", k=KC)

        rec_sb = later(1)
        gates = [sb(f"gates{i}", [P, (GATES + 1) * HG]) for i in range(2)]
        prods = [sb(f"prods{i}", [P, 2 * HG]) for i in range(2)]
        tanh_c = [sb(f"tanh_c{i}", [P, HG]) for i in range(2)]
        h_sb = sb("h_sb", [P, KC, GROUP])
        y_t = later(2).rearrange("p (c t) -> p c t", t=TOK)
        y_sb = later(3)

        ps_rec = psum("ps_rec")
        ps_gate = [psum("ps_gate0"), psum("ps_gate1")]
        ps_prep = [psum("ps_prep0"), psum("ps_prep1")]
        ps_y = psum("ps_y")

        cond_loaded, small_loaded, consts_loaded = sem("cond_loaded"), sem("small_loaded"), sem("consts_loaded")
        w1_loaded, up_loaded, down_loaded = sem("w1_loaded"), sem("up_loaded"), sem("down_loaded")
        wh_loaded = [sem(f"wh_loaded{k}") for k in range(KC)]
        wx_loaded = sem("wx_loaded")
        w2_loaded = [sem(f"w2_loaded{i}") for i in range(KC)]
        x_loaded, y_stored = sem("x_loaded"), sem("y_stored")
        cleared, vecs_turned, vecs_ready = sem("cleared"), sem("vecs_turned"), sem("vecs_ready")
        ln_step, ln_var, ln_root, ln_done = sem("ln_step"), sem("ln_var"), sem("ln_root"), sem("ln_done")
        cond_turned, state_turned, cond_ready = sem("cond_turned"), sem("state_turned"), sem("cond_ready")
        hid_mm, hid_ready = sem("hid_mm"), sem("hid_ready")
        up_turned, up_ready = sem("up_turned"), sem("up_ready")
        ada_mm = [sem(f"ada_mm{i}") for i in range(KC)]
        ada_taken = [sem(f"ada_taken{i}") for i in range(2)]
        ada_turned, ada_ready = sem("ada_turned"), sem("ada_ready")
        wh_halved, wh_part1, wh_rest1, wh_part2, wh_split = (
            sem("wh_halved"), sem("wh_part1"), sem("wh_rest1"), sem("wh_part2"), sem("wh_split"))
        gx_scaled = sem("gx_scaled")
        prep_mm, prep_taken = sem("prep_mm"), sem("prep_taken")
        y_turned, y_taken = sem("y_turned"), sem("y_taken")
        rec_mm, rec_taken = sem("rec_mm"), [sem("rec_taken0"), sem("rec_taken1")]
        gate_mm = [sem("gate_mm0"), sem("gate_mm1")]
        gates_done = [sem("gates_done0"), sem("gates_done1")]
        prods_done = [sem("prods_done0"), sem("prods_done1")]
        c_done = [sem("c_done0"), sem("c_done1")]
        tanh_c_done = [sem("tanh_c_done0"), sem("tanh_c_done1")]
        h_full = [sem("h_full0"), sem("h_full1")]
        h_rest = [sem("h_rest0"), sem("h_rest1")]
        h_ready = [sem("h_ready0"), sem("h_ready1")]
        y_added = sem("y_added")

        h_bits = h_sb[:].bitcast(BF16).rearrange("p k (c e) -> p k c e", e=2)

        def half_of(tile, part):
            return [tile[:, HC * hf:HC * hf + HC, part * B:part * B + B] for hf in range(2)]

        h2 = half_of(h_sb, 0)
        h2_hi = half_of(h_bits[:, :, :, 1], 0)
        rest1 = half_of(h_sb, 1)
        rest1_hi = half_of(h_bits[:, :, :, 1], 1)
        rest2 = half_of(h_sb, 2)

        def by_chunk(ap):
            return ap.rearrange("p (c b) -> p c b", b=B)

        def slot_value(m16, k):
            return m16 + (k if k < SLOTS else BT)

        block = ctx.enter_context(nc.Block())

        @block.sync
        def _(sp):
            sp.dma_start(cond_sb[:], cond).then_inc(cond_loaded, 16)
            row = 0
            for src in (ln_gamma, ln_beta, bias1, bias_g):
                rows = src.shape[0] // P
                sp.dma_start(vec_rows[row:row + rows], src.rearrange("(c p) -> c p", p=P)).then_inc(small_loaded, 16)
                row += rows
            sp.dma_start(w1_sb, w1.rearrange("(k p) l -> p k l", p=P)).then_inc(w1_loaded, 16)
            w2_view = w2.rearrange("(k p) o -> p k o", p=P)
            COLS = D * R // KC
            for dc in range(KC):
                sp.dma_start(w2_sb[dc][:], w2_view[:, :, dc * COLS:dc * COLS + COLS]).then_inc(w2_loaded[dc], 16)
            with sp.Fori(1, 4) as q:
                for dc in range(KC):
                    sp.wait_ge(ada_mm[dc], q)
                    sp.dma_start(w2_sb[dc][:], w2_view[:, :, bass.ds(q * (D * R) + dc * COLS, COLS)]).then_inc(w2_loaded[dc], 16)

            x_view = x.rearrange("b t d -> t b d")
            out_view = out.rearrange("b t d -> t b d")

            def load_x(n):
                sp.dma_start(x_sb[:], x_view[bass.ds(n * BT, BT)]).then_inc(x_loaded, 16)

            def store_y(n):
                sp.wait_ge(y_taken, n * 16 + 16)
                sp.dma_start(out_view[bass.ds(n * BT, BT)], y_sb).then_inc(y_stored, 16)

            load_x(0)
            sp.wait_ge(prep_mm, 1)
            load_x(1)
            with sp.Fori(1, NB - 1) as n:
                sp.wait_ge(prep_mm, n * 16 + 1)
                load_x(n + 1)
                store_y(n - 1)
            store_y(NB - 2)
            store_y(NB - 1)
            sp.wait_ge(y_stored, NB * 16)

        @block.gpsimd
        def _(pool):
            for k in range(KC):
                pool.wait_ge(wh_part1, k + 1)
                nc.gpsimd.tensor_tensor(wx_sb[:, k], wx_sb[:, k], wh_parts[:, 0, k], ALU.subtract).then_inc(wh_rest1, 1)
                pool.wait_ge(wh_part2, k + 1)
                pool.wait_ge(wh_rest1, k + 1)
                nc.gpsimd.tensor_tensor(wh_parts[:, 2, k], wx_sb[:, k], wh_parts[:, 1, k], ALU.subtract).then_inc(wh_split, 1)
            pool.wait_ge(wh_split, KC)
            pool.dma_start(wx_sb[:], wx.rearrange("(k p) g -> p k g", p=P)).then_inc(wx_loaded, 16)

        @block.scalar
        def _(act):
            wh_view = wh.rearrange("(k p) g -> p k g", p=P)
            act.dma_start(ident[:], ident_in).then_inc(consts_loaded, 16)
            act.dma_start(fold[:], fold_in).then_inc(consts_loaded, 16)
            act.dma_start(mask[:], mask_in).then_inc(consts_loaded, 16)
            act.dma_start(bias2_sb[:], bias2.rearrange("(q c p r) -> p q c r", q=4, c=KC, r=R)).then_inc(consts_loaded, 16)
            act.dma_start(up_raw, base_up.rearrange("(k p) l -> p k l", p=P)).then_inc(up_loaded, 16)
            for k in range(KC):
                act.dma_start(wx_sb[:, k], wh_view[:, k]).then_inc(wh_loaded[k], 16)
            act.dma_start(down_sb[:], base_down.rearrange("(k p) l -> p k l", p=P)).then_inc(down_loaded, 16)

            act.wait_ge(ln_var, 1)
            nc.scalar.activation(stat[:, 3:4], stat[:, 2:3], ACT.Sqrt).then_inc(ln_root, 1)

            SIG = (GATES - 1) * D

            def split_wh(k):
                act.wait_ge(wh_loaded[k], 16)
                nc.scalar.mul(wx_sb[:, k, 0:SIG], wx_sb[:, k, 0:SIG], 0.5).then_inc(wh_halved, 1)
                act.wait_ge(wh_halved, k + 1)
                nc.scalar.copy(wh_parts[:, 0, k], wx_sb[:, k]).then_inc(wh_part1, 1)
                act.wait_ge(wh_rest1, k + 1)
                nc.scalar.copy(wh_parts[:, 1, k], wx_sb[:, k]).then_inc(wh_part2, 1)

            split_wh(0)
            act.wait_ge(vecs_ready, 1)
            act.wait_ge(hid_mm, 1)
            for l in range(KC):
                nc.scalar.activation(hid_t[:, l], ps_prep[0][:, l * B:l * B + B], ACT.Gelu,
                                     bias=bias1_t[:, l:l + 1]).then_inc(hid_ready, 1)
            for k in range(1, KC):
                split_wh(k)

            def gelu_slot(m16, k):
                i = k - 3
                act.wait_ge(prep_mm, slot_value(m16, k))
                nc.scalar.activation(mid_t[:, 2 * i:2 * i + 2].rearrange("p c t -> p (c t)"),
                                     ps_prep[k % 2][:, 0:2 * TOK], ACT.Gelu).then_inc(prep_taken, 1)

            def step(t, s, prepare):
                act.wait_ge(rec_mm, t + 1)
                nc.scalar.copy(rec_sb[:, 0:FLAT], ps_rec[:, 0:FLAT]).then_inc(rec_taken[0], 1)
                for hf in range(2):
                    act.wait_ge(gate_mm[hf], t + 1)
                    nc.scalar.activation(gates[hf][:, 0:GATES * HG], ps_gate[hf][:, 0:GATES * HG], ACT.Tanh,
                                         scale=0.5).then_inc(gates_done[hf], 1)
                for hf in range(2):
                    act.wait_ge(c_done[hf], t + 1)
                    nc.scalar.activation(tanh_c[hf][:], gates[hf][:, GATES * HG:], ACT.Tanh,
                                         scale=0.5).then_inc(tanh_c_done[hf], 1)
                if prepare and s in (3, 4):
                    gelu_slot(t - s + BT, s)

            for k in (3, 4):
                gelu_slot(0, k)
            for s in range(BT):
                step(s, s, True)
            with act.Fori(BT, T - BT, 2 * BT) as t0:
                for s in range(2 * BT):
                    step(t0 + s, s % BT, True)
            for s in range(BT):
                step(T - BT + s, s, False)

        @block.tensor
        def _(pe):
            nc_mm = nc.tensor.matmul
            turn = nc.tensor.transpose
            pe.wait_ge(consts_loaded, 16 * 4)
            pe.wait_ge(cond_loaded, 16)
            for c in range(KC):
                last = turn(ps_gate[1][:, c * B:c * B + B], cond_sb[:, c * P:c * P + P], ident[0:B, 0:B])
            last.then_inc(state_turned, 1)
            pe.wait_ge(small_loaded, 16 * 4)
            turn(ps_prep[1][:, 0:VECS], vec_rows[:], ident[0:VECS, 0:VECS]).then_inc(vecs_turned, 1)
            pe.wait_ge(ln_done, 1)
            for c in range(KC):
                last = turn(ps_gate[0][:, c * B:c * B + B], cond_n[:, c * P:c * P + P], ident[0:B, 0:B])
            last.then_inc(cond_turned, 1)
            pe.wait_ge(w1_loaded, 16)
            pe.wait_ge(cond_ready, KC)
            for l in range(KC):
                for k in range(KC):
                    last = nc_mm(ps_prep[0][:, l * B:l * B + B], w1_sb[:, k, l * P:l * P + P], cond_t[:, k],
                                 start=(k == 0), stop=(k == KC - 1))
            last.then_inc(hid_mm, 1)
            pe.wait_ge(up_loaded, 16)
            pe.wait_ge(vecs_ready, 1)
            for l in range(KC):
                bank = (ps_prep[1], ps_y)[l % 2]
                if l >= 2:
                    pe.wait_ge(up_ready, l - 1)
                for k in range(KC):
                    last = turn(bank[:, k * P:k * P + P], up_raw[:, k, l * P:l * P + P], ident[:])
                last.then_inc(up_turned, 1)
            pe.wait_ge(hid_ready, KC)

            def adapters(q, dc, fresh):
                pe.wait_ge(w2_loaded[dc], 16 * q + 16)
                if not fresh:
                    pe.wait_ge(ada_taken[dc % 2], 2 * q + dc // 2)
                tile = w2_sb[dc][:].rearrange("p k (d r) -> p k d r", r=R)
                for r in range(R):
                    for k in range(KC):
                        last = nc_mm(ps_gate[dc % 2][:, r * B:r * B + B], tile[:, k, :, r], hid_t[:, k],
                                     start=(k == 0), stop=(k == KC - 1))
                last.then_inc(ada_mm[dc], 1)

            for dc in range(KC):
                adapters(0, dc, dc < 2)
            with pe.Fori(1, 4) as q:
                for dc in range(KC):
                    adapters(q, dc, False)
            for bank in range(2):
                pe.wait_ge(ada_taken[bank], 8)
            pe.wait_ge(up_ready, KC)
            for i, (q, bank) in enumerate(((0, ps_prep[1]), (3, ps_y))):
                for c in range(KC):
                    last = turn(bank[0:BR, c * P:c * P + P], ada[:, q, c, :], ident[:])
                last.then_inc(ada_turned, 1)

            def prep(m16, k, first=False):
                need = {1: m16, 2: m16 + 1, 3: m16 + 2, 5: m16 + 4, 6: m16 + 5, 8: m16 + 7}.get(k, m16 + k - 2)
                if not (first and k == 1) and k not in (4, 7, 9):
                    pe.wait_ge(prep_taken, need)
                bank = ps_prep[k % 2]
                par = prep.parity
                if k == 1:
                    pe.wait_ge(x_loaded, m16 + 16)
                    for c in range(KC):
                        last = turn(bank[:, c * P:c * P + P], x_sb[:, c * P:c * P + P], ident[:])
                elif k == 2:
                    for c in range(KC):
                        last = nc_mm(bank[0:BR, 0:TOK], ada[:, 2, c], x_t[:, c], start=(c == 0), stop=(c == KC - 1))
                elif k in (3, 4):
                    for i in range(2):
                        l = 2 * (k - 3) + i
                        dst = bank[:, i * TOK:i * TOK + TOK]
                        for c in range(KC):
                            nc_mm(dst, down_sb[:, c, l * P:l * P + P], x_t[:, c], start=(c == 0), stop=False)
                        last = nc_mm(dst, b2_t[:, l * P:l * P + P], u_m[:], start=False, stop=True)
                elif k == 5:
                    for c in range(KC):
                        last = nc_mm(bank[0:BR, 0:TOK], ada[:, 1, c], mid_t[:, c], start=(c == 0), stop=(c == KC - 1))
                elif k in (6, 7):
                    for i in range(2):
                        l = 2 * (k - 6) + i
                        dst = bank[:, i * TOK:i * TOK + TOK]
                        for c in range(KC):
                            nc_mm(dst, up_t[:, c, l * P:l * P + P], mid_t[:, c], start=(c == 0), stop=False)
                        last = nc_mm(dst, a1_t[:, l * P:l * P + P], v_m[:], start=False, stop=True)
                else:
                    hf, j = divmod(k - 8, GATES)
                    for i in range(HC):
                        col = j * D + (HC * hf + i) * P
                        for c in range(KC):
                            last = nc_mm(bank[:, i * TOK:i * TOK + TOK], wx_sb[:, c, col:col + P], x1_t[par][:, c],
                                         start=(c == 0), stop=(c == KC - 1))
                last.then_inc(prep_mm, 1 if k < SLOTS else 2)

            def turn_y(t0):
                pe.wait_ge(y_added, t0 + BT)
                for c in range(KC):
                    last = turn(ps_y[:, c * P:c * P + P], y_t[:, c], ident[:])
                last.then_inc(y_turned, 16)

            def recur(t):
                for hf in range(2):
                    pe.wait_ge(h_ready[hf], t + 1)
                    for c in range(HC * hf, HC * hf + HC):
                        for w in range(PARTS):
                            for j in range(GATES):
                                rows = slice(GROUP * j, GROUP * j + GROUP)
                                last = nc_mm(ps_rec[rows, :], h_bits[:, c, :, 1], wh_parts[:, w, c, j * D:j * D + D],
                                             start=(c == 0 and w == 0), stop=(c == KC - 1 and w == PARTS - 1),
                                             tile_position=(0, GROUP * j))
                last.then_inc(rec_mm, 1)

            def gate_inputs(t, s, par):
                for hf in range(2):
                    nc_mm(ps_gate[hf][:, 0:GATES * HG], ident[:], xw[par][:, s, hf], start=True, stop=True)
                for hf in range(2):
                    pe.wait_ge(rec_taken[hf], t + 1)
                    dst = ps_gate[hf][:, 0:GATES * HG].rearrange("p (j c b) -> p j c b", j=GATES, b=B)
                    for i in range(HC):
                        c = HC * hf + i
                        last = nc_mm(dst[:, :, i, :], rec_sb[:, c * P:c * P + P], fold[:],
                                     start=False, stop=True, skip_group_check=True)
                    last.then_inc(gate_mm[hf], 1)

            def step(t, s, par, prepare, output):
                recur(t)
                gate_inputs(t, s, par)
                if s == 0 and output:
                    turn_y(t - BT)
                if s > 0 and prepare:
                    prep.parity = 1 - par
                    prep(t - s + BT, s)

            pe.wait_ge(ada_ready, 2)
            pe.wait_ge(down_loaded, 16)
            prep.parity = 0
            for k in range(1, 8):
                prep(0, k, first=True)
            pe.wait_ge(gx_scaled, 2)
            for k in range(8, SLOTS + 1):
                prep(0, k, first=True)
            pe.wait_ge(prep_taken, BT)
            pe.wait_ge(wh_split, KC)
            for s in range(BT):
                step(s, s, 0, True, False)
            with pe.Fori(BT, T - BT, 2 * BT) as t0:
                for s in range(2 * BT):
                    if s % BT == 0:
                        pe.wait_ge(prep_taken, t0 + s + BT)
                    step(t0 + s, s % BT, 1 - s // BT, True, True)
            pe.wait_ge(prep_taken, T)
            for s in range(BT):
                step(T - BT + s, s, 1, False, True)
            pe.wait_ge(y_taken, T - BT)
            turn_y(T - BT)

        @block.vector
        def _(dve):
            stt = nc.vector.scalar_tensor_tensor
            tt = nc.vector.tensor_tensor
            ts = nc.vector.tensor_scalar
            nc.vector.memset(h_sb[:], 0.0).then_inc(cleared, 1)
            for hf in range(2):
                nc.vector.memset(gates[hf][:], 0.0).then_inc(cleared, 1)

            dve.wait_ge(cond_loaded, 16)
            nc.vector.reduce_sum(stat[:, 0:1], cond_sb[:], AX.X).then_inc(ln_step, 1)
            dve.wait_ge(ln_step, 1)
            ts(stat[:, 0:1], stat[:, 0:1], 1.0 / D, None, ALU.mult).then_inc(ln_step, 1)
            dve.wait_ge(ln_step, 2)
            ts(cond_n[:], cond_sb[:], stat[:, 0:1], None, ALU.subtract).then_inc(ln_step, 1)
            dve.wait_ge(ln_step, 3)
            tt(cond_sq[:], cond_n[:], cond_n[:], ALU.mult).then_inc(ln_step, 1)
            dve.wait_ge(ln_step, 4)
            nc.vector.reduce_sum(stat[:, 1:2], cond_sq[:], AX.X).then_inc(ln_step, 1)
            dve.wait_ge(ln_step, 5)
            ts(stat[:, 2:3], stat[:, 1:2], 1.0 / D, LN_EPS, ALU.mult, ALU.add).then_inc(ln_var, 1)
            dve.wait_ge(ln_var, 1)
            dve.wait_ge(ln_root, 1)
            nc.vector.reciprocal(stat[:, 4:5], stat[:, 3:4]).then_inc(ln_step, 1)
            dve.wait_ge(ln_step, 6)
            stt(stat[:, 5:6], stat[:, 2:3], stat[:, 4:5], stat[:, 3:4], ALU.mult, ALU.add).then_inc(ln_step, 1)
            dve.wait_ge(ln_step, 7)
            ts(stat[:, 6:7], stat[:, 5:6], 0.5, None, ALU.mult).then_inc(ln_step, 1)
            dve.wait_ge(ln_step, 8)
            nc.vector.reciprocal(stat[:, 7:8], stat[:, 6:7]).then_inc(ln_step, 1)
            dve.wait_ge(ln_step, 9)
            ts(cond_n[:], cond_n[:], stat[:, 7:8], None, ALU.mult).then_inc(ln_done, 1)

            dve.wait_ge(cleared, 3)
            dve.wait_ge(state_turned, 1)
            for hf in range(2):
                src = ps_gate[1][:, hf * HG:hf * HG + HG].rearrange("p (c b) -> p c b", b=B)
                ts(h2[hf], src, 2.0, None, ALU.mult).then_inc(h_full[hf], 1)
                dve.wait_ge(h_full[hf], 1)
                tt(rest1[hf], h2[hf], h2_hi[hf], ALU.subtract).then_inc(h_rest[hf], 1)
                dve.wait_ge(h_rest[hf], 1)
                tt(rest2[hf], rest1[hf], rest1_hi[hf], ALU.subtract).then_inc(h_ready[hf], 1)

            dve.wait_ge(vecs_turned, 1)
            nc.vector.tensor_copy(vecs_t[:], ps_prep[1][:, 0:VECS]).then_inc(vecs_ready, 1)
            dve.wait_ge(vecs_ready, 1)
            dve.wait_ge(cond_turned, 1)
            for c in range(KC):
                ts(cond_t[:, c], ps_gate[0][:, c * B:c * B + B], gamma_t[:, c:c + 1], beta_t[:, c:c + 1],
                   ALU.mult, ALU.add).then_inc(cond_ready, 1)
            for l in range(KC):
                dve.wait_ge(up_turned, l + 1)
                nc.vector.tensor_copy(up_t[:, l], (ps_prep[1], ps_y)[l % 2][:]).then_inc(up_ready, 1)

            dve.wait_ge(consts_loaded, 16 * 4)
            ts(gate_bias[:, :, GATES - 1], gate_bias[:, :, GATES - 1], 2.0, None, ALU.mult).then_inc(gx_scaled, 1)

            with dve.Fori(0, 4) as q:
                for dc in range(KC):
                    dve.wait_ge(ada_mm[dc], q + 1)
                    bias = bias2_sb[:, bass.ds(q, 1), dc].rearrange("p q r -> p (q r)").unsqueeze(2).broadcast_to([P, R, B])
                    dst = ada[:, bass.ds(q, 1), dc].rearrange("p q (r b) -> p (q r) b", b=B)
                    tt(dst, ps_gate[dc % 2][:, 0:BR].rearrange("p (r b) -> p r b", b=B), bias, ALU.add).then_inc(ada_taken[dc % 2], 1)
            dve.wait_ge(ada_turned, 1)
            nc.vector.tensor_copy(a1_t[:], ps_prep[1][0:BR, :]).then_inc(ada_ready, 1)
            dve.wait_ge(ada_turned, 2)
            nc.vector.tensor_copy(b2_t[:], ps_y[0:BR, :]).then_inc(ada_ready, 1)

            def prep(m16, k, par):
                if k in (3, 4):
                    return
                dve.wait_ge(prep_mm, slot_value(m16, k))
                bank = ps_prep[k % 2]
                if k == 1:
                    last = nc.vector.tensor_copy(x_t[:].rearrange("p c t -> p (c t)"), bank[:])
                elif k in (2, 5):
                    last = tt((u_m if k == 2 else v_m)[:], bank[0:BR, 0:TOK], mask[:], ALU.mult)
                elif k in (6, 7):
                    c = 2 * (k - 6)
                    last = stt(x1_t[par][:, c:c + 2].rearrange("p c t -> p (c t)"),
                               x_t[:, c:c + 2].rearrange("p c t -> p (c t)"), 2.0, bank[:, 0:2 * TOK],
                               ALU.mult, ALU.add)
                else:
                    hf, j = divmod(k - 8, GATES)
                    dst = xw[par][:, :, hf, j * HG:j * HG + HG].rearrange("p t (c b) -> p c t b", b=B)
                    src = bank[:, 0:HC * TOK].rearrange("p (c t b) -> p c t b", c=HC, b=B)
                    bias = gate_bias[:, hf, j].unsqueeze(2).unsqueeze(3).broadcast_to([P, HC, BT, B])
                    last = tt(dst, src, bias, ALU.add)
                last.then_inc(prep_taken, 1 if k < SLOTS else 2)

            def take_y(t0, first=False):
                dve.wait_ge(y_turned, t0 + 16)
                if not first:
                    dve.wait_ge(y_stored, t0)
                nc.vector.tensor_copy(y_sb, ps_y[:]).then_inc(y_taken, 16)

            def step(t, s, par, prepare, output, second=False):
                dve.wait_ge(rec_taken[0], t + 1)
                nc.vector.tensor_copy(rec_sb[:, FLAT:], ps_rec[:, FLAT:]).then_inc(rec_taken[1], 1)
                for hf in range(2):
                    g = gates[hf]
                    dve.wait_ge(gates_done[hf], t + 1)
                    stt(prods[hf][:], g[:, 0:2 * HG], 1.0, g[:, 3 * HG:5 * HG], ALU.add, ALU.mult).then_inc(prods_done[hf], 1)
                    dve.wait_ge(prods_done[hf], t + 1)
                    stt(g[:, 4 * HG:], prods[hf][:, HG:], 0.5, prods[hf][:, 0:HG], ALU.mult, ALU.add).then_inc(c_done[hf], 1)
                for hf in range(2):
                    dve.wait_ge(tanh_c_done[hf], t + 1)
                    stt(h2[hf], by_chunk(gates[hf][:, 2 * HG:3 * HG]), 1.0, by_chunk(tanh_c[hf][:]),
                        ALU.add, ALU.mult).then_inc(h_full[hf], 1)
                    dve.wait_ge(h_full[hf], t + 2)
                    tt(rest1[hf], h2[hf], h2_hi[hf], ALU.subtract).then_inc(h_rest[hf], 1)
                    dve.wait_ge(h_rest[hf], t + 2)
                    tt(rest2[hf], rest1[hf], rest1_hi[hf], ALU.subtract).then_inc(h_ready[hf], 1)
                if s == 0 and output:
                    take_y(t - BT, first=second)
                stt(y_t[:, :, s * B:s * B + B], h_sb[:, :, 0:B], 0.5, x1_t[par][:, :, s * B:s * B + B],
                    ALU.mult, ALU.add).then_inc(y_added, 1)
                if s > 0 and prepare:
                    prep(t - s + BT, s, 1 - par)

            for k in range(1, 8):
                prep(0, k, 0)
            dve.wait_ge(wx_loaded, 16)
            ts(wx_sb[:, :, (GATES - 1) * D:], wx_sb[:, :, (GATES - 1) * D:], 2.0, None, ALU.mult).then_inc(gx_scaled, 1)
            dve.wait_ge(gx_scaled, 1)
            for k in range(8, SLOTS + 1):
                prep(0, k, 0)
            for s in range(BT):
                step(s, s, 0, True, False)
            with dve.Fori(BT, T - BT, 2 * BT) as t0:
                for s in range(2 * BT):
                    step(t0 + s, s % BT, 1 - s // BT, True, True)
            for s in range(BT):
                step(T - BT + s, s, 1, False, True)
            take_y(T - BT)


_INS = ['x', 'cond_1024', 'L0_cond_base_up', 'L0_cond_base_down', 'L0_cond_ln_gamma', 'L0_cond_ln_beta',
        'L0_cond_W1', 'L0_cond_bias1', 'L0_cond_W2', 'L0_cond_bias2', 'L1_cond_Wx', 'L1_cond_Wh', 'L1_cond_b']


def shape_constants(B, R):
    import numpy as np

    ident = np.eye(P, dtype=np.float32)
    fold = np.zeros((P, GATES * B), np.float32)
    for j in range(GATES):
        for part in range(PARTS):
            for b in range(B):
                fold[GROUP * j + part * B + b, j * B + b] = 1
    mask = (np.arange(B * R)[:, None] % B == np.arange(P)[None, :] % B).astype(np.float32)
    return {"ident": ident, "fold": fold, "mask": mask}


def kernel(**inputs):
    import numpy as _np
    import concourse.bacc as _bacc
    from concourse import mybir as _mybir
    from concourse.bass_utils import run_bass_kernel_spmd as _run

    nc = _bacc.Bacc("TRN2", target_bir_lowering=False, num_devices=1)
    arrays = {f"in_{name}_dram": _np.ascontiguousarray(inputs[name]) for name in _INS}
    B, T, D = inputs['x'].shape
    for name, a in shape_constants(B, inputs['L0_cond_W2'].shape[1] // (4 * D)).items():
        arrays[f"const_{name}_dram"] = a
    args = [nc.dram_tensor(n, a.shape, _mybir.dt.from_np(a.dtype), kind="ExternalInput").ap() for n, a in arrays.items()]
    args.append(nc.dram_tensor("out_0_dram", (B, T, D), _mybir.dt.float32, kind="ExternalOutput").ap())
    cond_residual_lstm(nc, *args)
    r = _run(nc, [arrays], core_ids=[0])
    return r.results[0]["out_0_dram"]
```

```python
from contextlib import ExitStack

import concourse.bass as bass
from concourse import mybir

P = 128
F32 = mybir.dt.float32
BF16 = mybir.dt.bfloat16
ALU = mybir.AluOpType
ACT = mybir.ActivationFunctionType
AX = mybir.AxisListType

BT = 16
GATES = 4
PARTS = 3
GROUP = 32
NG = P // GROUP
SLOTS = 15
LN_EPS = 1e-5


def folded(ap):
    return ap.rearrange("p (j k u) -> p k j u", j=NG, u=GROUP)


def by_fold(ap):
    return ap.rearrange("p (k j u) -> p k j u", j=NG, u=GROUP)


def cond_residual_lstm(nc, x, cond, base_up, base_down, ln_gamma, ln_beta, w1, bias1, w2, bias2,
                       wx, wh, bias_g, ident_in, pick_in, mask_in, out):
    B, T, D = x.shape
    KC = D // P
    HC = KC // 2
    NB = T // BT
    R = w2.shape[1] // (4 * D)
    RG = R // NG
    BR = B * R
    TOK = BT * B
    HG = HC * B
    HU = HC * GROUP
    assert TOK == P and D == 512 and KC == NG and NB % 2 == 0 and PARTS * B <= GROUP

    with ExitStack() as ctx:
        def sb(name, shape, dt=F32):
            return ctx.enter_context(nc.sbuf_tensor(name, shape, dt))

        def psum(name):
            return ctx.enter_context(nc.psum_tensor(name, [P, 512], F32))

        def sem(name):
            return ctx.enter_context(nc.semaphore(name))

        ident = sb("ident", [P, P])
        pick = sb("pick", [P, NG * B])
        mask = sb("mask", [BR, TOK])
        wh_parts = sb("wh_parts", [P, PARTS, KC, GATES * D], BF16)
        wx_sb = sb("wx_sb", [P, KC, GATES * D])
        down_sb = sb("down_sb", [P, KC, D])
        up_t = sb("up_t", [P, KC, D])
        ada = sb("ada", [P, 4, KC, BR])
        a1_t = sb("a1_t", [BR, D])
        b2_t = sb("b2_t", [BR, D])

        w2_sb = [sb(f"w2_sb{i}", [P, KC, D * R // KC]) for i in range(KC)]
        ada_row = [sb(f"ada_row{i}", [P, RG * P]) for i in range(2)]
        bias2_sb = sb("bias2_sb", [P, 4, KC, R])
        cond_sb = sb("cond_sb", [B, D])
        cond_n = sb("cond_n", [B, D])
        cond_f = sb("cond_f", [B, D])
        stat = sb("stat", [B, 12])
        VECS = (3 + GATES) * KC
        vec_rows = sb("vec_rows", [VECS, P])
        vecs_t = sb("vecs_t", [P, VECS])
        gamma_t, beta_t, bias1_t = (vecs_t[:, KC * i:KC * i + KC] for i in range(3))
        gate_bias = vecs_t[:, 3 * KC:].rearrange("p (g h c) -> p h g c", g=GATES, h=2)
        cond_t = sb("cond_t", [P, KC, B])
        hid_t = sb("hid_t", [P, KC, GROUP])

        x_sb = sb("x_sb", [TOK, D])
        pool_region = sb("pool_region", [P, 4 * D])
        w1_sb = pool_region[:].rearrange("p (k l) -> p k l", k=KC)

        def region(i):
            return pool_region[:, i * D:i * D + D]

        x1_t = [region(i).rearrange("p (c t) -> p c t", t=TOK) for i in range(2)]
        x_t = region(2).rearrange("p (c t) -> p c t", t=TOK)
        x_f = region(3)
        xw = [sb(f"xw{i}", [P, BT, 2, GATES * HG]) for i in range(2)]
        stages = [xw[i][:].rearrange("p t h g -> p (t h g)") for i in range(2)]
        up_raw = wx_sb[:, 0].rearrange("p (k l) -> p k l", k=KC)

        def later(i):
            return w2_sb[KC - 1 - i // 8][:].rearrange("p k c -> p (k c)")[:, (i % 8) * D:(i % 8) * D + D]

        a2_t = later(0)[0:BR]
        mid_t = later(0).rearrange("p (c t) -> p c t", t=TOK)
        y_t = later(2).rearrange("p (c t) -> p c t", t=TOK)
        y_sb = later(3)
        u_m, v_m = (later(i)[0:BR, 0:TOK] for i in (4, 5))

        pair = range(2)
        turned = [later(1)[:, i * GATES * HU:(i + 1) * GATES * HU] for i in pair]
        summed = [sb(f"summed{i}", [P, GATES * HG]) for i in pair]
        inputs = [sb(f"inputs{i}", [P, GATES * HG]) for i in pair]
        gates = [sb(f"gates{i}", [P, (GATES + 1) * HG]) for i in pair]
        prods = [sb(f"prods{i}", [P, 2 * HG]) for i in pair]
        tanh_c = [sb(f"tanh_c{i}", [P, HG]) for i in pair]
        h_sb = sb("h_sb", [P, KC, GROUP])

        ps_rec = [psum("ps_rec0"), psum("ps_rec1")]
        ps_prep = [psum("ps_prep0"), psum("ps_prep1")]
        ps_y = psum("ps_y")
        ps_ada = [psum("ps_ada0"), psum("ps_ada1")]
        ps_turn = psum("ps_turn")
        ps_rank, ps_mid, ps_x1 = ps_ada[0], ps_ada[1], ps_turn

        cond_loaded, small_loaded, consts_loaded = sem("cond_loaded"), sem("small_loaded"), sem("consts_loaded")
        w1_loaded, up_loaded, down_loaded = sem("w1_loaded"), sem("up_loaded"), sem("down_loaded")
        wh_loaded = [sem(f"wh_loaded{i}") for i in pair]
        wx_loaded = [sem(f"wx_loaded{i}") for i in pair]
        w2_loaded = [sem(f"w2_loaded{i}") for i in range(KC)]
        x_loaded, y_stored = sem("x_loaded"), sem("y_stored")
        cleared, vecs_turned, vecs_ready = sem("cleared"), sem("vecs_turned"), sem("vecs_ready")
        ln_step, ln_var, ln_root, ln_done = sem("ln_step"), sem("ln_var"), sem("ln_root"), sem("ln_done")
        cond_folded = sem("cond_folded")
        cond_turned, state_turned, cond_ready = sem("cond_turned"), sem("state_turned"), sem("cond_ready")
        hid_mm, hid_ready = sem("hid_mm"), sem("hid_ready")
        up_turned, up_ready = sem("up_turned"), sem("up_ready")
        ada_mm = [sem(f"ada_mm{i}") for i in range(KC)]
        ada_rows = [sem(f"ada_rows{i}") for i in range(KC)]
        ada_turned = [sem(f"ada_turned{i}") for i in range(KC)]
        ada_taken = [sem(f"ada_taken{i}") for i in range(KC)]
        rows_turned, rows_ready = sem("rows_turned"), sem("rows_ready")
        a2_turned, a2_ready = sem("a2_turned"), sem("a2_ready")
        wh_halved, wh_part1, wh_rest1, wh_part2, wh_split = (
            sem("wh_halved"), sem("wh_part1"), sem("wh_rest1"), sem("wh_part2"), sem("wh_split"))
        wx_folded, bias_doubled = sem("wx_folded"), sem("bias_doubled")
        prep_mm, prep_taken = sem("prep_mm"), sem("prep_taken")
        x_folded = sem("x_folded")
        y_turned, y_taken = sem("y_turned"), sem("y_taken")
        rec_mm = [sem(f"rec_mm{i}") for i in pair]
        turn_done = [sem(f"turn_done{i}") for i in pair]
        sum_done = [sem(f"sum_done{i}") for i in pair]
        inputs_done = [sem(f"inputs_done{i}") for i in pair]
        gates_done = [sem(f"gates_done{i}") for i in pair]
        prods_done = [sem(f"prods_done{i}") for i in pair]
        c_done = [sem(f"c_done{i}") for i in pair]
        tanh_c_done = [sem(f"tanh_c_done{i}") for i in pair]
        h_full = [sem(f"h_full{i}") for i in pair]
        h_rest = [sem(f"h_rest{i}") for i in pair]
        h_ready = [sem(f"h_ready{i}") for i in pair]
        y_added = sem("y_added")

        h_bits = h_sb[:].bitcast(BF16).rearrange("p k (c e) -> p k c e", e=2)

        def halves(tile, part):
            return [tile[:, HC * nh:HC * nh + HC, part * B:part * B + B] for nh in pair]

        h2, rest1, rest2 = (halves(h_sb, part) for part in range(PARTS))
        h2_hi, rest1_hi = (halves(h_bits[:, :, :, 1], part) for part in range(PARTS - 1))

        def by_chunk(ap):
            return ap.rearrange("p (c b) -> p c b", b=B)

        def slot_value(m16, k):
            return m16 + (k if k < SLOTS else BT)

        def rows_of_chunk(w, k):
            return w.rearrange("(j k u) g -> k j u g", k=KC, u=GROUP)[k]

        block = ctx.enter_context(nc.Block())

        @block.sync
        def _(sp):
            sp.dma_start(cond_sb[:], cond).then_inc(cond_loaded, 16)
            row = 0
            for src in (ln_gamma, ln_beta, bias1):
                sp.dma_start(vec_rows[row:row + KC], src.rearrange("(c p) -> c p", p=P)).then_inc(small_loaded, 16)
                row += KC
            for g in range(GATES):
                src = bias_g[g * D:g * D + D].rearrange("(j k u) -> k j u", k=KC, u=GROUP)
                sp.dma_start(vec_rows[row:row + KC], src).then_inc(small_loaded, 16)
                row += KC
            sp.dma_start(w1_sb, w1.rearrange("(k p) l -> p k l", p=P)).then_inc(w1_loaded, 16)
            w2_view = w2.rearrange("(k p) o -> p k o", p=P)
            COLS = D * R // KC
            for dc in range(KC):
                sp.dma_start(w2_sb[dc][:], w2_view[:, :, dc * COLS:dc * COLS + COLS]).then_inc(w2_loaded[dc], 16)
            with sp.Fori(1, 4) as q:
                for dc in range(KC):
                    sp.wait_ge(ada_mm[dc], q)
                    sp.dma_start(w2_sb[dc][:], w2_view[:, :, bass.ds(q * (D * R) + dc * COLS, COLS)]).then_inc(w2_loaded[dc], 16)

            x_view = x.rearrange("b t d -> t b d")
            out_view = out.rearrange("b t d -> t b d")

            def load_x(n):
                sp.dma_start(x_sb[:], x_view[bass.ds(n * BT, BT)]).then_inc(x_loaded, 16)

            def store_y(n):
                sp.wait_ge(y_taken, n * 16 + 16)
                sp.dma_start(out_view[bass.ds(n * BT, BT)], y_sb).then_inc(y_stored, 16)

            load_x(0)
            sp.wait_ge(x_folded, 16)
            load_x(1)
            with sp.Fori(1, NB - 1) as n:
                sp.wait_ge(x_folded, n * 16 + 16)
                load_x(n + 1)
                store_y(n - 1)
            store_y(NB - 2)
            store_y(NB - 1)
            sp.wait_ge(y_stored, NB * 16)

        @block.gpsimd
        def _(pool):
            for k in range(KC):
                st = stages[k % 2]
                pool.wait_ge(wh_part1, k + 1)
                nc.gpsimd.tensor_tensor(st, st, wh_parts[:, 0, k], ALU.subtract).then_inc(wh_rest1, 1)
                pool.wait_ge(wh_part2, k + 1)
                pool.wait_ge(wh_rest1, k + 1)
                nc.gpsimd.tensor_tensor(wh_parts[:, 2, k], st, wh_parts[:, 1, k], ALU.subtract).then_inc(wh_split, 1)

            def fold_x(m16):
                pool.wait_ge(x_loaded, m16 + 16)
                nc.gpsimd.tensor_copy(by_fold(x_f), folded(x_sb[:])).then_inc(x_folded, 16)

            pool.wait_ge(hid_mm, 1)
            fold_x(0)
            with pool.Fori(1, NB) as m:
                pool.wait_ge(prep_mm, m * 16 - 15)
                fold_x(m * 16)

        @block.scalar
        def _(act):
            SIG = (GATES - 1) * D
            act.dma_start(ident[:], ident_in).then_inc(consts_loaded, 16)
            act.dma_start(pick[:], pick_in).then_inc(consts_loaded, 16)
            act.dma_start(mask[:], mask_in).then_inc(consts_loaded, 16)
            act.dma_start(bias2_sb[:], bias2.rearrange("(q c p r) -> p q c r", q=4, c=KC, r=R)).then_inc(consts_loaded, 16)
            act.dma_start(up_raw, base_up.rearrange("(k p) l -> p k l", p=P)).then_inc(up_loaded, 16)
            for k in range(2):
                act.dma_start(stages[k], rows_of_chunk(wh, k)).then_inc(wh_loaded[k], 16)
            for k in range(KC):
                act.dma_start(down_sb[:, k], rows_of_chunk(base_down, k)).then_inc(down_loaded, 16)

            act.wait_ge(ln_var, 1)
            nc.scalar.activation(stat[:, 3:4], stat[:, 2:3], ACT.Sqrt).then_inc(ln_root, 1)
            act.wait_ge(vecs_ready, 1)
            act.wait_ge(hid_mm, 1)
            act.wait_ge(cleared, 4)
            for l in range(KC):
                nc.scalar.activation(hid_t[:, l, 0:B], ps_prep[0][:, l * B:l * B + B], ACT.Gelu,
                                     bias=bias1_t[:, l:l + 1]).then_inc(hid_ready, 1)

            for k in range(KC):
                st = stages[k % 2]
                act.wait_ge(wh_loaded[k % 2], 16 * (k // 2) + 16)
                nc.scalar.mul(st[:, 0:SIG], st[:, 0:SIG], 0.5).then_inc(wh_halved, 1)
                act.wait_ge(wh_halved, k + 1)
                nc.scalar.copy(wh_parts[:, 0, k], st).then_inc(wh_part1, 1)
                act.wait_ge(wh_rest1, k + 1)
                nc.scalar.copy(wh_parts[:, 1, k], st).then_inc(wh_part2, 1)
                if k >= 1:
                    act.wait_ge(wh_split, k)
                    nxt = k + 1
                    if nxt < KC:
                        act.dma_start(stages[nxt % 2], rows_of_chunk(wh, nxt)).then_inc(wh_loaded[nxt % 2], 16)
                    else:
                        act.dma_start(stages[0], rows_of_chunk(wx, 0)).then_inc(wx_loaded[0], 16)
            act.wait_ge(wh_split, KC)
            act.dma_start(stages[1], rows_of_chunk(wx, 1)).then_inc(wx_loaded[1], 16)
            act.wait_ge(up_turned, KC)
            for k in range(KC):
                st = stages[k % 2]
                act.wait_ge(wx_loaded[k % 2], 16 * (k // 2) + 16)
                for g in range(GATES):
                    cols = slice(g * D, g * D + D)
                    nc.scalar.mul(by_fold(wx_sb[:, k, cols]), folded(st[:, cols]),
                                  2.0 if g == GATES - 1 else 1.0).then_inc(wx_folded, 1)
                if k + 2 < KC:
                    act.wait_ge(wx_folded, GATES * (k + 1))
                    act.dma_start(st, rows_of_chunk(wx, k + 2)).then_inc(wx_loaded[k % 2], 16)

            def gelu_slot(m16):
                act.wait_ge(prep_mm, m16 + 4)
                nc.scalar.activation(mid_t.rearrange("p c t -> p (c t)"), ps_mid[:], ACT.Gelu).then_inc(prep_taken, 2)

            def step(t, s, prepare):
                for nh in pair:
                    act.wait_ge(inputs_done[nh], t + 1)
                    nc.scalar.activation(gates[nh][:, 0:GATES * HG], inputs[nh][:], ACT.Tanh,
                                         scale=0.5).then_inc(gates_done[nh], 1)
                    act.wait_ge(c_done[nh], t + 1)
                    nc.scalar.activation(tanh_c[nh][:], gates[nh][:, GATES * HG:], ACT.Tanh,
                                         scale=0.5).then_inc(tanh_c_done[nh], 1)
                if prepare and s == 4:
                    gelu_slot(t - s + BT)

            gelu_slot(0)
            for s in range(BT):
                step(s, s, True)
            with act.Fori(BT, T - BT, 2 * BT) as t0:
                for s in range(2 * BT):
                    step(t0 + s, s % BT, True)
            for s in range(BT):
                step(T - BT + s, s, False)

        @block.tensor
        def _(pe):
            nc_mm = nc.tensor.matmul
            turn = nc.tensor.transpose
            pe.wait_ge(consts_loaded, 16 * 4)
            pe.wait_ge(small_loaded, 16 * (3 + GATES))
            turn(ps_prep[1][:, 0:VECS], vec_rows[:], ident[0:VECS, 0:VECS]).then_inc(vecs_turned, 1)
            pe.wait_ge(cond_folded, 1)
            for c in range(KC):
                last = turn(ps_ada[1][:, c * B:c * B + B], cond_f[:, c * P:c * P + P], ident[0:B, 0:B])
            last.then_inc(state_turned, 1)
            pe.wait_ge(ln_done, 1)
            for c in range(KC):
                last = turn(ps_ada[0][:, c * B:c * B + B], cond_n[:, c * P:c * P + P], ident[0:B, 0:B])
            last.then_inc(cond_turned, 1)
            pe.wait_ge(w1_loaded, 16)
            pe.wait_ge(cond_ready, KC)
            for l in range(KC):
                for k in range(KC):
                    last = nc_mm(ps_prep[0][:, l * B:l * B + B], w1_sb[:, k, l * P:l * P + P], cond_t[:, k],
                                 start=(k == 0), stop=(k == KC - 1))
            last.then_inc(hid_mm, 1)
            pe.wait_ge(up_loaded, 16)
            pe.wait_ge(vecs_ready, 1)
            for l in range(KC):
                bank = (ps_prep[1], ps_y)[l % 2]
                if l >= 2:
                    pe.wait_ge(up_ready, l - 1)
                for k in range(KC):
                    last = turn(bank[:, k * P:k * P + P], up_raw[:, k, l * P:l * P + P], ident[:])
                last.then_inc(up_turned, 1)

            def before(sems, q, dc, first):
                if dc >= 2:
                    pe.wait_ge(sems[dc - 2], q + 1)
                elif not first:
                    pe.wait_ge(sems[dc + 2], q)

            def ada_products(q, dc, first):
                pe.wait_ge(w2_loaded[dc], 16 * q + 16)
                before(ada_rows, q, dc, first)
                tile = w2_sb[dc][:].rearrange("p k (d r) -> p k r d", r=R)
                for k in range(KC):
                    for g in range(NG):
                        last = nc_mm(ps_ada[dc % 2][GROUP * g:GROUP * g + GROUP, 0:RG * P], hid_t[:, k],
                                     tile[:, k, RG * g:RG * g + RG], start=(k == 0), stop=(k == KC - 1),
                                     tile_position=(0, GROUP * g))
                last.then_inc(ada_mm[dc], 1)

            def ada_turn(q, dc, first):
                pe.wait_ge(ada_rows[dc], q + 1)
                before(ada_taken, q, dc, first)
                bank = (ps_turn, ps_prep[0])[dc % 2]
                for r in range(RG):
                    last = nc_mm(bank[:, r * NG * B:(r + 1) * NG * B], ada_row[dc % 2][:, r * P:r * P + P], pick[:],
                                 start=True, stop=True)
                last.then_inc(ada_turned[dc], 1)

            def ada_matrix(q, first):
                ada_products(q, 0, first)
                for dc in range(1, KC):
                    ada_products(q, dc, first)
                    ada_turn(q, dc - 1, first)
                ada_turn(q, KC - 1, first)

            pe.wait_ge(hid_ready, KC)
            ada_matrix(0, True)
            with pe.Fori(1, 4) as q:
                ada_matrix(q, False)
            for dc in range(KC):
                pe.wait_ge(ada_taken[dc], 4)
            pe.wait_ge(up_ready, KC)
            for q, bank in ((2, ps_turn), (0, ps_prep[1]), (3, ps_y)):
                for c in range(KC):
                    last = turn(bank[0:BR, c * P:c * P + P], ada[:, q, c, :], ident[:])
                last.then_inc(rows_turned, 1)
            pe.wait_ge(rows_ready, 1)
            for c in range(KC):
                last = turn(ps_ada[0][:, c * BR:c * BR + BR], a2_t[:, c * P:c * P + P], ident[0:BR, 0:BR])
            last.then_inc(a2_turned, 1)

            def low_rank_sum(bank, weights, rhs, rank_weights, rank_rhs, lo, hi):
                for i in range(lo, hi):
                    l, c = divmod(i, KC + 1)
                    dst, cols = bank[:, l * TOK:l * TOK + TOK], slice(l * P, l * P + P)
                    if c < KC:
                        last = nc_mm(dst, weights[:, c, cols], rhs[:, c], start=(c == 0), stop=False)
                    else:
                        last = nc_mm(dst, rank_weights[:, cols], rank_rhs, start=False, stop=True)
                return last

            def prep(m16, k, par, first=False):
                need = {1: m16, 2: m16 + 1, 3: m16 + 2, 5: m16 + 4, 6: m16 + 5, 8: m16 + 7}.get(k, m16 + k - 2)
                if not (first and k == 1) and k not in (4, 7, 9):
                    pe.wait_ge(prep_taken, need)
                CUTS = (0, KC, 2 * KC + 4, KC * (KC + 1))
                if k == 1:
                    pe.wait_ge(x_folded, m16 + 16)
                    for c in range(KC):
                        last = turn(ps_prep[1][:, c * P:c * P + P], x_f[:, c * P:c * P + P], ident[:])
                elif k in (2, 3, 4):
                    if k == 2:
                        for c in range(KC):
                            nc_mm(ps_rank[0:BR, 0:TOK], ada[:, 2, c], x_t[:, c], start=(c == 0), stop=(c == KC - 1))
                    last = low_rank_sum(ps_mid, down_sb, x_t, b2_t, u_m, CUTS[k - 2], CUTS[k - 1])
                elif k in (5, 6, 7):
                    if k == 5:
                        for c in range(KC):
                            nc_mm(ps_rank[0:BR, 0:TOK], ada[:, 1, c], mid_t[:, c], start=(c == 0), stop=(c == KC - 1))
                    last = low_rank_sum(ps_x1, up_t, mid_t, a1_t, v_m, CUTS[k - 5], CUTS[k - 4])
                else:
                    nh, g = divmod(k - 8, GATES)
                    for i in range(HC):
                        col = g * D + (HC * nh + i) * P
                        for c in range(KC):
                            last = nc_mm(ps_prep[k % 2][:, i * TOK:i * TOK + TOK], wx_sb[:, c, col:col + P],
                                         x1_t[par][:, c], start=(c == 0), stop=(c == KC - 1))
                last.then_inc(prep_mm, 1 if k < SLOTS else 2)

            def turn_y(t0):
                pe.wait_ge(y_added, t0 + BT)
                for c in range(KC):
                    last = turn(ps_y[:, c * P:c * P + P], y_t[:, c], ident[:])
                last.then_inc(y_turned, 16)

            def recur(t):
                def products(c, nh):
                    for w in range(PARTS):
                        rhs = wh_parts[:, w, c].rearrange("p (g c) -> p g c", g=GATES)
                        for j in range(NG):
                            u0 = P * j + HU * nh
                            last = nc_mm(ps_rec[nh][GROUP * j:GROUP * j + GROUP, 0:GATES * HU],
                                         h_bits[:, c, :, 1], rhs[:, :, u0:u0 + HU],
                                         start=(c == 0 and w == 0), stop=(c == KC - 1 and w == PARTS - 1),
                                         tile_position=(0, GROUP * j))
                    return last

                pe.wait_ge(h_ready[0], t + 1)
                products(0, 0)
                products(1, 0)
                products(0, 1)
                pe.wait_ge(h_ready[1], t + 1)
                products(2, 0)
                products(3, 0).then_inc(rec_mm[0], 1)
                for c in range(1, KC - 1):
                    products(c, 1)
                products(KC - 1, 1).then_inc(rec_mm[1], 1)

            def step(t, s, par, prepare, output):
                recur(t)
                if s == 0 and output:
                    turn_y(t - BT)
                if s > 0 and prepare:
                    prep(t - s + BT, s, 1 - par)

            pe.wait_ge(rows_ready, 3)
            pe.wait_ge(a2_ready, 1)
            pe.wait_ge(down_loaded, 16 * KC)
            for k in range(1, 8):
                prep(0, k, 0, first=True)
            pe.wait_ge(wx_folded, GATES * KC)
            for k in range(8, SLOTS + 1):
                prep(0, k, 0, first=True)
            pe.wait_ge(wh_split, KC)
            for s in range(BT):
                step(s, s, 0, True, False)
            with pe.Fori(BT, T - BT, 2 * BT) as t0:
                for s in range(2 * BT):
                    step(t0 + s, s % BT, 1 - s // BT, True, True)
            for s in range(BT):
                step(T - BT + s, s, 1, False, True)
            pe.wait_ge(y_taken, T - BT)
            turn_y(T - BT)

        @block.vector
        def _(dve):
            stt = nc.vector.scalar_tensor_tensor
            tt = nc.vector.tensor_tensor
            ts = nc.vector.tensor_scalar
            nc.vector.memset(h_sb[:], 0.0).then_inc(cleared, 1)
            nc.vector.memset(hid_t[:], 0.0).then_inc(cleared, 1)
            for nh in pair:
                nc.vector.memset(gates[nh][:], 0.0).then_inc(cleared, 1)

            dve.wait_ge(cond_loaded, 16)
            nc.vector.tensor_copy(by_fold(cond_f[:]), folded(cond_sb[:])).then_inc(cond_folded, 1)
            nc.vector.reduce_sum(stat[:, 0:1], cond_sb[:], AX.X).then_inc(ln_step, 1)
            dve.wait_ge(ln_step, 1)
            ts(stat[:, 0:1], stat[:, 0:1], 1.0 / D, None, ALU.mult).then_inc(ln_step, 1)
            dve.wait_ge(ln_step, 2)
            ts(cond_n[:], cond_sb[:], stat[:, 0:1], None, ALU.subtract).then_inc(ln_step, 1)
            dve.wait_ge(ln_step, 3)
            tt(cond_sb[:], cond_n[:], cond_n[:], ALU.mult).then_inc(ln_step, 1)
            dve.wait_ge(ln_step, 4)
            nc.vector.reduce_sum(stat[:, 1:2], cond_sb[:], AX.X).then_inc(ln_step, 1)
            dve.wait_ge(ln_step, 5)
            ts(stat[:, 2:3], stat[:, 1:2], 1.0 / D, LN_EPS, ALU.mult, ALU.add).then_inc(ln_var, 1)
            dve.wait_ge(ln_var, 1)
            dve.wait_ge(ln_root, 1)
            nc.vector.reciprocal(stat[:, 4:5], stat[:, 3:4]).then_inc(ln_step, 1)
            dve.wait_ge(ln_step, 6)
            stt(stat[:, 5:6], stat[:, 2:3], stat[:, 4:5], stat[:, 3:4], ALU.mult, ALU.add).then_inc(ln_step, 1)
            dve.wait_ge(ln_step, 7)
            ts(stat[:, 6:7], stat[:, 5:6], 0.5, None, ALU.mult).then_inc(ln_step, 1)
            dve.wait_ge(ln_step, 8)
            nc.vector.reciprocal(stat[:, 7:8], stat[:, 6:7]).then_inc(ln_step, 1)
            dve.wait_ge(ln_step, 9)
            ts(cond_n[:], cond_n[:], stat[:, 7:8], None, ALU.mult).then_inc(ln_done, 1)

            dve.wait_ge(vecs_turned, 1)
            nc.vector.tensor_copy(vecs_t[:], ps_prep[1][:, 0:VECS]).then_inc(vecs_ready, 1)
            dve.wait_ge(vecs_ready, 1)
            dve.wait_ge(cond_turned, 1)
            for c in range(KC):
                ts(cond_t[:, c], ps_ada[0][:, c * B:c * B + B], gamma_t[:, c:c + 1], beta_t[:, c:c + 1],
                   ALU.mult, ALU.add).then_inc(cond_ready, 1)

            dve.wait_ge(cleared, 4)
            dve.wait_ge(state_turned, 1)
            for nh in pair:
                ts(h2[nh], by_chunk(ps_ada[1][:, nh * HG:nh * HG + HG]), 2.0, None, ALU.mult).then_inc(h_full[nh], 1)
                dve.wait_ge(h_full[nh], 1)
                tt(rest1[nh], h2[nh], h2_hi[nh], ALU.subtract).then_inc(h_rest[nh], 1)
                dve.wait_ge(h_rest[nh], 1)
                tt(rest2[nh], rest1[nh], rest1_hi[nh], ALU.subtract).then_inc(h_ready[nh], 1)

            for l in range(KC):
                dve.wait_ge(up_turned, l + 1)
                nc.vector.tensor_copy(by_fold(up_t[:, l]), folded((ps_prep[1], ps_y)[l % 2][:])).then_inc(up_ready, 1)

            ts(gate_bias[:, :, GATES - 1], gate_bias[:, :, GATES - 1], 2.0, None, ALU.mult).then_inc(bias_doubled, 1)
            dve.wait_ge(bias_doubled, 1)

            dve.wait_ge(consts_loaded, 16 * 4)

            def ada_copy(q, dc, first):
                dve.wait_ge(ada_mm[dc], q + 1)
                if dc >= 2:
                    dve.wait_ge(ada_turned[dc - 2], q + 1)
                elif not first:
                    dve.wait_ge(ada_turned[dc + 2], q)
                nc.vector.tensor_copy(ada_row[dc % 2][:], ps_ada[dc % 2][:, 0:RG * P]).then_inc(ada_rows[dc], 1)

            def ada_store(q, dc):
                dve.wait_ge(ada_turned[dc], q + 1)
                src = (ps_turn, ps_prep[0])[dc % 2][:, 0:BR].rearrange("p (r g b) -> p r g b", r=RG, b=B)
                dst = ada[:, bass.ds(q, 1), dc].rearrange("p q (g r b) -> p (q r) g b", g=NG, b=B)
                bias = bias2_sb[:, bass.ds(q, 1), dc].rearrange("p q (g r) -> p (q r) g", g=NG)
                tt(dst, src, bias.unsqueeze(3).broadcast_to([P, RG, NG, B]), ALU.add).then_inc(ada_taken[dc], 1)

            def ada_matrix(q, first):
                ada_copy(q, 0, first)
                for dc in range(1, KC):
                    ada_copy(q, dc, first)
                    ada_store(q, dc - 1)
                ada_store(q, KC - 1)

            ada_matrix(0, True)
            with dve.Fori(1, 4) as q:
                ada_matrix(q, False)
            dve.wait_ge(rows_turned, 1)
            nc.vector.tensor_copy(by_fold(a2_t), folded(ps_turn[0:BR, :])).then_inc(rows_ready, 1)
            dve.wait_ge(rows_turned, 2)
            nc.vector.tensor_copy(by_fold(a1_t[:]), folded(ps_prep[1][0:BR, :])).then_inc(rows_ready, 1)
            dve.wait_ge(rows_turned, 3)
            nc.vector.tensor_copy(b2_t[:], ps_y[0:BR, :]).then_inc(rows_ready, 1)
            dve.wait_ge(a2_turned, 1)
            nc.vector.tensor_copy(ada[:, 2].rearrange("p c r -> p (c r)"), ps_ada[0][:, 0:KC * BR]).then_inc(a2_ready, 1)

            def prep(m16, k, par):
                if k in (3, 4, 6):
                    return
                dve.wait_ge(prep_mm, slot_value(m16, k))
                if k == 1:
                    last = nc.vector.tensor_copy(x_t.rearrange("p c t -> p (c t)"), ps_prep[1][:])
                elif k in (2, 5):
                    last = tt(u_m if k == 2 else v_m, ps_rank[0:BR, 0:TOK], mask[:], ALU.mult)
                elif k == 7:
                    last = stt(x1_t[par].rearrange("p c t -> p (c t)"), x_t.rearrange("p c t -> p (c t)"), 2.0,
                               ps_x1[:], ALU.mult, ALU.add)
                else:
                    nh, g = divmod(k - 8, GATES)
                    dst = xw[par][:, :, nh, g * HG:g * HG + HG].rearrange("p t (c b) -> p c t b", b=B)
                    src = ps_prep[k % 2][:, 0:HC * TOK].rearrange("p (c t b) -> p c t b", c=HC, b=B)
                    bias = gate_bias[:, nh, g].unsqueeze(2).unsqueeze(3).broadcast_to([P, HC, BT, B])
                    last = tt(dst, src, bias, ALU.add)
                last.then_inc(prep_taken, 2 if k in (7, SLOTS) else 1)

            def take_y(t0, first=False):
                dve.wait_ge(y_turned, t0 + 16)
                if not first:
                    dve.wait_ge(y_stored, t0)
                nc.vector.tensor_copy(folded(y_sb), by_fold(ps_y[:])).then_inc(y_taken, 16)

            def turn_half(t, nh):
                dve.wait_ge(rec_mm[nh], t + 1)
                nc.vector.transpose(turned[nh], ps_rec[nh][:, 0:GATES * HU]).then_inc(turn_done[nh], 1)

            def sum_parts(t, nh):
                dve.wait_ge(turn_done[nh], t + 1)
                src = turned[nh].rearrange("p (g q b) -> p g b q", b=B, q=GROUP // B)[:, :, :, 0:PARTS]
                nc.vector.tensor_reduce(summed[nh][:].rearrange("p (g b) -> p g b", b=B), src, AX.X,
                                        ALU.add).then_inc(sum_done[nh], 1)

            def add_projection(t, s, par, nh):
                dve.wait_ge(sum_done[nh], t + 1)
                tt(inputs[nh][:], summed[nh][:], xw[par][:, s, nh], ALU.add).then_inc(inputs_done[nh], 1)

            def products(t, nh):
                dve.wait_ge(gates_done[nh], t + 1)
                g = gates[nh]
                stt(prods[nh][:], g[:, 0:2 * HG], 1.0, g[:, 3 * HG:5 * HG], ALU.add, ALU.mult).then_inc(prods_done[nh], 1)

            def cell(t, nh):
                dve.wait_ge(prods_done[nh], t + 1)
                stt(gates[nh][:, 4 * HG:], prods[nh][:, HG:], 0.5, prods[nh][:, 0:HG], ALU.mult, ALU.add).then_inc(c_done[nh], 1)

            def hidden(t, nh):
                dve.wait_ge(tanh_c_done[nh], t + 1)
                stt(h2[nh], by_chunk(gates[nh][:, 2 * HG:3 * HG]), 1.0, by_chunk(tanh_c[nh][:]),
                    ALU.add, ALU.mult).then_inc(h_full[nh], 1)

            def remainder1(t, nh):
                dve.wait_ge(h_full[nh], t + 2)
                tt(rest1[nh], h2[nh], h2_hi[nh], ALU.subtract).then_inc(h_rest[nh], 1)

            def remainder2(t, nh):
                dve.wait_ge(h_rest[nh], t + 2)
                tt(rest2[nh], rest1[nh], rest1_hi[nh], ALU.subtract).then_inc(h_ready[nh], 1)

            def step(t, s, par, prepare, output, second=False):
                turn_half(t, 0)
                sum_parts(t, 0)
                add_projection(t, s, par, 0)
                turn_half(t, 1)
                products(t, 0)
                cell(t, 0)
                sum_parts(t, 1)
                hidden(t, 0)
                add_projection(t, s, par, 1)
                remainder1(t, 0)
                remainder2(t, 0)
                products(t, 1)
                cell(t, 1)
                hidden(t, 1)
                remainder1(t, 1)
                remainder2(t, 1)
                if s == 0 and output:
                    take_y(t - BT, first=second)
                stt(y_t[:, :, s * B:s * B + B], h_sb[:, :, 0:B], 0.5, x1_t[par][:, :, s * B:s * B + B],
                    ALU.mult, ALU.add).then_inc(y_added, 1)
                if s > 0 and prepare:
                    prep(t - s + BT, s, 1 - par)

            for k in range(1, SLOTS + 1):
                prep(0, k, 0)
            dve.wait_ge(prep_taken, BT)
            for s in range(BT):
                step(s, s, 0, True, False)
            with dve.Fori(BT, T - BT, 2 * BT) as t0:
                for s in range(2 * BT):
                    if s % BT == 0:
                        dve.wait_ge(prep_taken, t0 + s + BT)
                    step(t0 + s, s % BT, 1 - s // BT, True, True)
            dve.wait_ge(prep_taken, T)
            for s in range(BT):
                step(T - BT + s, s, 1, False, True)
            take_y(T - BT)


_INS = ['x', 'cond_1024', 'L0_cond_base_up', 'L0_cond_base_down', 'L0_cond_ln_gamma', 'L0_cond_ln_beta',
        'L0_cond_W1', 'L0_cond_bias1', 'L0_cond_W2', 'L0_cond_bias2', 'L1_cond_Wx', 'L1_cond_Wh', 'L1_cond_b']


def shape_constants(B, R):
    import numpy as np

    ident = np.eye(P, dtype=np.float32)
    pick = np.zeros((P, NG * B), np.float32)
    for g in range(NG):
        for b in range(B):
            pick[GROUP * g + b, g * B + b] = 1
    mask = (np.arange(B * R)[:, None] % B == np.arange(P)[None, :] % B).astype(np.float32)
    return {"ident": ident, "pick": pick, "mask": mask}


def kernel(**inputs):
    import numpy as _np
    import concourse.bacc as _bacc
    from concourse import mybir as _mybir
    from concourse.bass_utils import run_bass_kernel_spmd as _run

    nc = _bacc.Bacc("TRN2", target_bir_lowering=False, num_devices=1)
    arrays = {f"in_{name}_dram": _np.ascontiguousarray(inputs[name]) for name in _INS}
    B, T, D = inputs['x'].shape
    for name, a in shape_constants(B, inputs['L0_cond_W2'].shape[1] // (4 * D)).items():
        arrays[f"const_{name}_dram"] = a
    args = [nc.dram_tensor(n, a.shape, _mybir.dt.from_np(a.dtype), kind="ExternalInput").ap() for n, a in arrays.items()]
    args.append(nc.dram_tensor("out_0_dram", (B, T, D), _mybir.dt.float32, kind="ExternalOutput").ap())
    cond_residual_lstm(nc, *args)
    r = _run(nc, [arrays], core_ids=[0])
    return r.results[0]["out_0_dram"]
```

```python
from contextlib import ExitStack

import concourse.bass as bass
from concourse import mybir

P = 128
F32 = mybir.dt.float32
BF16 = mybir.dt.bfloat16
ALU = mybir.AluOpType
ACT = mybir.ActivationFunctionType
AX = mybir.AxisListType

BT = 16
GATES = 4
PARTS = 3
GROUP = 32
NG = P // GROUP
WARM = 4
LN_EPS = 1e-5


UNITS = (("u", 4), ("mid", 20), ("v", 4), ("x1", 20)) + tuple((f"wx{i}", 8) for i in range(2 * GATES))
SLOT_SIZES = (6, 6, 6, 6, 8, 8, 8, 7, 7, 7, 7, 7, 7, 7, 7, 8)
MATMULS = [(unit, i) for unit, size in UNITS for i in range(size)]
SLOT = [MATMULS[sum(SLOT_SIZES[:k]):sum(SLOT_SIZES[:k + 1])] for k in range(BT)]
LAST = {(unit, size - 1): unit for unit, size in UNITS}
FINISHED = [[LAST[m] for m in SLOT[k] if m in LAST] for k in range(BT)]
MID_SLOT, V_SLOT, X1_SLOT = ([unit in f for f in FINISHED].index(True) for unit in ("mid", "v", "x1"))
TAKEN = {unit: (BT if i == len(UNITS) - 1 else i + 1) for i, (unit, _) in enumerate(UNITS)}


def folded(ap):
    return ap.rearrange("p (j k u) -> p k j u", j=NG, u=GROUP)


def by_fold(ap):
    return ap.rearrange("p (k j u) -> p k j u", j=NG, u=GROUP)


def cond_residual_lstm(nc, x, cond, base_up, base_down, ln_gamma, ln_beta, w1, bias1, w2, bias2,
                       wx, wh, bias_g, ident_in, pick_in, mask_in, out):
    B, T, D = x.shape
    KC = D // P
    HC = KC // 2
    NB = T // BT
    R = w2.shape[1] // (4 * D)
    RG = R // NG
    BR = B * R
    TOK = BT * B
    NDMA = NG * GROUP // B
    Y_STEP = 1
    HG = HC * B
    HU = HC * GROUP
    assert TOK == P and D == 512 and KC == NG and NB % 2 == 0 and PARTS * B <= GROUP

    with ExitStack() as ctx:
        def sb(name, shape, dt=F32):
            return ctx.enter_context(nc.sbuf_tensor(name, shape, dt))

        def psum(name):
            return ctx.enter_context(nc.psum_tensor(name, [P, 512], F32))

        def sem(name):
            return ctx.enter_context(nc.semaphore(name))

        ident = sb("ident", [P, P])
        pick = sb("pick", [P, NG * B])
        mask = sb("mask", [BR, TOK])
        wh_parts = sb("wh_parts", [P, PARTS, KC, GATES * D], BF16)
        wx_sb = sb("wx_sb", [P, KC, GATES * D])
        down_sb = sb("down_sb", [P, KC, D])
        up_t = sb("up_t", [P, KC, D])
        ada = sb("ada", [P, 4, KC, BR])
        a1_t = sb("a1_t", [BR, D])
        b2_t = sb("b2_t", [BR, D])

        w2_sb = [sb(f"w2_sb{i}", [P, KC, D * R // KC]) for i in range(KC)]
        ada_row = [sb(f"ada_row{i}", [P, RG * P]) for i in range(2)]
        bias2_sb = sb("bias2_sb", [P, 4, KC, R])
        cond_sb = sb("cond_sb", [B, D])
        cond_n = b2_t[0:B]
        cond_f = a1_t[0:B]
        stat = sb("stat", [B, 12])
        VECS = (3 + GATES) * KC
        vec_rows = sb("vec_rows", [VECS, P])
        vecs_t = sb("vecs_t", [P, VECS])
        gamma_t, beta_t, bias1_t = (vecs_t[:, KC * i:KC * i + KC] for i in range(3))
        gate_bias = vecs_t[:, 3 * KC:].rearrange("p (g h c) -> p h g c", g=GATES, h=2)
        cond_t = sb("cond_t", [P, KC, B])
        hid_t = sb("hid_t", [P, KC, GROUP])

        x_sb = sb("x_sb", [P, D])
        prep_region = sb("prep_region", [P, 4 * D])
        w1_sb = prep_region[:].rearrange("p (k l) -> p k l", k=KC)

        def region(i):
            return prep_region[:, i * D:i * D + D]

        x1_t = [region(i).rearrange("p (c t) -> p c t", t=TOK) for i in range(2)]
        x_t = region(2).rearrange("p (c t) -> p c t", t=TOK)
        mid_t = region(3).rearrange("p (c t) -> p c t", t=TOK)
        a2_t = region(0)[0:BR]
        u_m, v_m = (sb(name, [BR, TOK])[:] for name in ("u_m", "v_m"))
        xw = [sb(f"xw{i}", [P, BT, 2, GATES * HG]) for i in range(2)]
        stages = [xw[i][:].rearrange("p t h g -> p (t h g)") for i in range(2)]
        up_raw = wx_sb[:, 0].rearrange("p (k l) -> p k l", k=KC)

        def later(i):
            return w2_sb[KC - 1 - i // 8][:].rearrange("p k c -> p (k c)")[:, (i % 8) * D:(i % 8) * D + D]

        y_t = [later(i).rearrange("p (c t) -> p c t", t=TOK) for i in (2, 6)]
        y_sb = later(3)

        pair = range(2)
        turned = [later(1)[:, i * GATES * HU:(i + 1) * GATES * HU] for i in pair]
        summed = [sb(f"summed{i}", [P, GATES * HG]) for i in pair]
        inputs = [sb(f"inputs{i}", [P, GATES * HG]) for i in pair]
        gates = [sb(f"gates{i}", [P, (GATES + 1) * HG]) for i in pair]
        prods = [sb(f"prods{i}", [P, 2 * HG]) for i in pair]
        tanh_c = [sb(f"tanh_c{i}", [P, HG]) for i in pair]
        h_sb = sb("h_sb", [P, KC, GROUP])

        ps_rec = [psum("ps_rec0"), psum("ps_rec1")]
        ps_prep = [psum("ps_prep0"), psum("ps_prep1")]
        ps_mid = psum("ps_mid")
        ps_ada = [psum("ps_ada0"), psum("ps_ada1")]
        ps_turn = psum("ps_turn")
        rank_x1_banks = ps_ada[0], ps_turn
        first_banks = ps_rec

        cond_loaded, small_loaded, consts_loaded = sem("cond_loaded"), sem("small_loaded"), sem("consts_loaded")
        w1_loaded, up_loaded, down_loaded = sem("w1_loaded"), sem("up_loaded"), sem("down_loaded")
        wh_loaded = [sem(f"wh_loaded{i}") for i in pair]
        wx_loaded = [sem(f"wx_loaded{i}") for i in pair]
        w2_loaded = [sem(f"w2_loaded{i}") for i in range(KC)]
        x_loaded, y_stored = sem("x_loaded"), sem("y_stored")
        cleared, vecs_turned, vecs_ready = sem("cleared"), sem("vecs_turned"), sem("vecs_ready")
        ln_step, ln_var, ln_root, ln_done = sem("ln_step"), sem("ln_var"), sem("ln_root"), sem("ln_done")
        cond_folded = sem("cond_folded")
        cond_turned, state_turned, cond_ready = sem("cond_turned"), sem("state_turned"), sem("cond_ready")
        hid_mm, hid_ready = sem("hid_mm"), sem("hid_ready")
        up_turned, up_ready = sem("up_turned"), sem("up_ready")
        ada_mm = [sem(f"ada_mm{i}") for i in range(KC)]
        ada_rows = [sem(f"ada_rows{i}") for i in range(KC)]
        ada_turned = [sem(f"ada_turned{i}") for i in range(KC)]
        ada_taken = [sem(f"ada_taken{i}") for i in range(KC)]
        rows_turned, rows_ready = sem("rows_turned"), sem("rows_ready")
        a2_turned, a2_ready = sem("a2_turned"), sem("a2_ready")
        wh_halved, wh_part1, wh_rest1, wh_part2, wh_split = (
            sem("wh_halved"), sem("wh_part1"), sem("wh_rest1"), sem("wh_part2"), sem("wh_split"))
        wx_folded, bias_doubled = sem("wx_folded"), sem("bias_doubled")
        prep_mm, prep_taken = sem("prep_mm"), sem("prep_taken")
        x_turned = sem("x_turned")
        y_turned = sem("y_turned")
        rec_mm = [sem(f"rec_mm{i}") for i in pair]
        turn_done = [sem(f"turn_done{i}") for i in pair]
        sum_done = [sem(f"sum_done{i}") for i in pair]
        inputs_done = [sem(f"inputs_done{i}") for i in pair]
        gates_done = [sem(f"gates_done{i}") for i in pair]
        prods_done = [sem(f"prods_done{i}") for i in pair]
        c_done = [sem(f"c_done{i}") for i in pair]
        tanh_c_done = [sem(f"tanh_c_done{i}") for i in pair]
        h_full = [sem(f"h_full{i}") for i in pair]
        h_rest = [sem(f"h_rest{i}") for i in pair]
        h_ready = [sem(f"h_ready{i}") for i in pair]
        y_added = sem("y_added")

        h_bits = h_sb[:].bitcast(BF16).rearrange("p k (c e) -> p k c e", e=2)

        def halves(tile, part):
            return [tile[:, HC * nh:HC * nh + HC, part * B:part * B + B] for nh in pair]

        h2, rest1, rest2 = (halves(h_sb, part) for part in range(PARTS))
        h2_hi, rest1_hi = (halves(h_bits[:, :, :, 1], part) for part in range(PARTS - 1))

        def by_chunk(ap):
            return ap.rearrange("p (c b) -> p c b", b=B)

        def blocks_of_32(ap):
            return ap.rearrange("p (a k u) -> p k a u", k=KC, u=GROUP)

        def rows_of_chunk(w, k):
            return w.rearrange("(j k u) g -> k j u g", k=KC, u=GROUP)[k]

        block = ctx.enter_context(nc.Block())

        @block.sync
        def _(sp):
            sp.dma_start(cond_sb[:], cond).then_inc(cond_loaded, 16)
            row = 0
            for src in (ln_gamma, ln_beta, bias1):
                sp.dma_start(vec_rows[row:row + KC], src.rearrange("(c p) -> c p", p=P)).then_inc(small_loaded, 16)
                row += KC
            for g in range(GATES):
                src = bias_g[g * D:g * D + D].rearrange("(j k u) -> k j u", k=KC, u=GROUP)
                sp.dma_start(vec_rows[row:row + KC], src).then_inc(small_loaded, 16)
                row += KC
            QT = GROUP // B

            def parts(dram, tile, n):
                for j in range(NG):
                    rows = dram[:, bass.ds(n * BT, BT), P * j:P * j + P].rearrange("b (a t) d -> t b a d", t=QT)
                    for t in range(QT):
                        lo = GROUP * j + B * t
                        yield rows[t], tile[lo:lo + B].rearrange("p (a d) -> p a d", d=P)

            def load_x(n):
                for src, dst in parts(x, x_sb, n):
                    sp.dma_start(dst, src).then_inc(x_loaded, 16)

            def store_y(n):
                sp.wait_ge(y_turned, n * 16 + 16)
                for dst, src in parts(out, y_sb, n):
                    sp.dma_start(dst, src).then_inc(y_stored, 16)

            sp.dma_start(w1_sb, w1.rearrange("(k p) l -> p k l", p=P)).then_inc(w1_loaded, 16)
            load_x(0)
            w2_view = w2.rearrange("(k p) o -> p k o", p=P)
            COLS = D * R // KC

            def load_w2(dc, q):
                sp.dma_start(w2_sb[dc][:], w2_view[:, :, bass.ds(q * (D * R) + dc * COLS, COLS)]).then_inc(w2_loaded[dc], 16)

            for dc in range(KC):
                load_w2(dc, 2)
            for dc in range(KC):
                sp.wait_ge(ada_mm[dc], 1)
                load_w2(dc, 3)
            with sp.Fori(0, 2) as q:
                for dc in range(KC):
                    sp.wait_ge(ada_mm[dc], q + 2)
                    load_w2(dc, q)

            sp.wait_ge(x_turned, 16)
            load_x(1)
            with sp.Fori(1, NB - 1) as n:
                sp.wait_ge(x_turned, n * 16 + 16)
                load_x(n + 1)
                store_y(n - 1)
            store_y(NB - 2)
            store_y(NB - 1)
            sp.wait_ge(y_stored, NB * 16 * NDMA)

        @block.gpsimd
        def _(pool):
            for k in range(KC):
                st = stages[k % 2]
                pool.wait_ge(wh_part1, k + 1)
                nc.gpsimd.tensor_tensor(st, st, wh_parts[:, 0, k], ALU.subtract).then_inc(wh_rest1, 1)
                pool.wait_ge(wh_part2, k + 1)
                pool.wait_ge(wh_rest1, k + 1)
                nc.gpsimd.tensor_tensor(wh_parts[:, 2, k], st, wh_parts[:, 1, k], ALU.subtract).then_inc(wh_split, 1)

        @block.scalar
        def _(act):
            SIG = (GATES - 1) * D
            act.dma_start(ident[:], ident_in).then_inc(consts_loaded, 16)
            act.dma_start(pick[:], pick_in).then_inc(consts_loaded, 16)
            act.dma_start(mask[:], mask_in).then_inc(consts_loaded, 16)
            act.dma_start(bias2_sb[:], bias2.rearrange("(q c p r) -> p q c r", q=4, c=KC, r=R)).then_inc(consts_loaded, 16)
            act.dma_start(up_raw, base_up.rearrange("(k p) l -> p k l", p=P)).then_inc(up_loaded, 16)
            for k in range(2):
                act.dma_start(stages[k], rows_of_chunk(wh, k)).then_inc(wh_loaded[k], 16)
            for k in range(KC):
                act.dma_start(down_sb[:, k], rows_of_chunk(base_down, k)).then_inc(down_loaded, 16)

            act.wait_ge(ln_var, 1)
            nc.scalar.activation(stat[:, 3:4], stat[:, 2:3], ACT.Sqrt).then_inc(ln_root, 1)
            act.wait_ge(vecs_ready, 1)
            act.wait_ge(hid_mm, 1)
            act.wait_ge(cleared, 4)
            for l in range(KC):
                nc.scalar.activation(hid_t[:, l, 0:B], ps_prep[0][:, l * B:l * B + B], ACT.Gelu,
                                     bias=bias1_t[:, l:l + 1]).then_inc(hid_ready, 1)

            def gelu_slot(m16):
                act.wait_ge(prep_mm, m16 + MID_SLOT + 1)
                nc.scalar.activation(mid_t.rearrange("p c t -> p (c t)"), ps_mid[:], ACT.Gelu).then_inc(prep_taken, 1)

            for k in range(KC):
                if k == KC - 1:
                    gelu_slot(0)
                st = stages[k % 2]
                act.wait_ge(wh_loaded[k % 2], 16 * (k // 2) + 16)
                nc.scalar.mul(st[:, 0:SIG], st[:, 0:SIG], 0.5).then_inc(wh_halved, 1)
                act.wait_ge(wh_halved, k + 1)
                nc.scalar.copy(wh_parts[:, 0, k], st).then_inc(wh_part1, 1)
                act.wait_ge(wh_rest1, k + 1)
                nc.scalar.copy(wh_parts[:, 1, k], st).then_inc(wh_part2, 1)
                if k >= 1:
                    act.wait_ge(wh_split, k)
                    nxt = k + 1
                    if nxt < KC:
                        act.dma_start(stages[nxt % 2], rows_of_chunk(wh, nxt)).then_inc(wh_loaded[nxt % 2], 16)
                    else:
                        act.dma_start(stages[0], rows_of_chunk(wx, 0)).then_inc(wx_loaded[0], 16)
            act.wait_ge(wh_split, KC)
            act.dma_start(stages[1], rows_of_chunk(wx, 1)).then_inc(wx_loaded[1], 16)
            act.wait_ge(up_turned, KC)
            for k in range(KC):
                st = stages[k % 2]
                act.wait_ge(wx_loaded[k % 2], 16 * (k // 2) + 16)
                for g in range(GATES):
                    cols = slice(g * D, g * D + D)
                    nc.scalar.mul(by_fold(wx_sb[:, k, cols]), folded(st[:, cols]),
                                  2.0 if g == GATES - 1 else 1.0).then_inc(wx_folded, 1)
                if k + 2 < KC:
                    act.wait_ge(wx_folded, GATES * (k + 1))
                    act.dma_start(st, rows_of_chunk(wx, k + 2)).then_inc(wx_loaded[k % 2], 16)

            def step(t, s, prepare):
                for nh in pair:
                    act.wait_ge(inputs_done[nh], t + 1)
                    nc.scalar.activation(gates[nh][:, 0:GATES * HG], inputs[nh][:], ACT.Tanh,
                                         scale=0.5).then_inc(gates_done[nh], 1)
                    act.wait_ge(c_done[nh], t + 1)
                    nc.scalar.activation(tanh_c[nh][:], gates[nh][:, GATES * HG:], ACT.Tanh,
                                         scale=0.5).then_inc(tanh_c_done[nh], 1)
                if prepare and s == MID_SLOT:
                    gelu_slot(t - s + BT)

            for s in range(BT):
                step(s, s, True)
            with act.Fori(BT, T - BT, 2 * BT) as t0:
                for s in range(2 * BT):
                    step(t0 + s, s % BT, True)
            for s in range(BT):
                step(T - BT + s, s, False)

        @block.tensor
        def _(pe):
            nc_mm = nc.tensor.matmul
            turn = nc.tensor.transpose
            pe.wait_ge(consts_loaded, 16 * 4)
            pe.wait_ge(small_loaded, 16 * (3 + GATES))
            turn(ps_prep[1][:, 0:VECS], vec_rows[:], ident[0:VECS, 0:VECS]).then_inc(vecs_turned, 1)
            pe.wait_ge(cond_folded, 1)
            for c in range(KC):
                last = turn(ps_ada[1][:, c * B:c * B + B], cond_f[:, c * P:c * P + P], ident[0:B, 0:B])
            last.then_inc(state_turned, 1)
            pe.wait_ge(ln_done, 1)
            for c in range(KC):
                last = turn(ps_ada[0][:, c * B:c * B + B], cond_n[:, c * P:c * P + P], ident[0:B, 0:B])
            last.then_inc(cond_turned, 1)
            pe.wait_ge(w1_loaded, 16)
            pe.wait_ge(cond_ready, KC)
            for l in range(KC):
                for k in range(KC):
                    last = nc_mm(ps_prep[0][:, l * B:l * B + B], w1_sb[:, k, l * P:l * P + P], cond_t[:, k],
                                 start=(k == 0), stop=(k == KC - 1))
            last.then_inc(hid_mm, 1)
            pe.wait_ge(up_loaded, 16)
            pe.wait_ge(vecs_ready, 1)
            for l in range(KC):
                bank = (ps_prep[1], ps_mid)[l % 2]
                if l >= 2:
                    pe.wait_ge(up_ready, l - 1)
                for k in range(KC):
                    last = turn(bank[:, k * P:k * P + P], up_raw[:, k, l * P:l * P + P], ident[:])
                last.then_inc(up_turned, 1)

            def before(sems, r, dc):
                if dc >= 2:
                    pe.wait_ge(sems[dc - 2], r + 1)
                elif not (isinstance(r, int) and r == 0):
                    pe.wait_ge(sems[dc + 2], r)

            def ada_products(r, dc):
                pe.wait_ge(w2_loaded[dc], 16 * r + 16)
                before(ada_rows, r, dc)
                tile = w2_sb[dc][:].rearrange("p k (d r) -> p k r d", r=R)
                for k in range(KC):
                    for g in range(NG):
                        last = nc_mm(ps_ada[dc % 2][GROUP * g:GROUP * g + GROUP, 0:RG * P], hid_t[:, k],
                                     tile[:, k, RG * g:RG * g + RG], start=(k == 0), stop=(k == KC - 1),
                                     tile_position=(0, GROUP * g))
                last.then_inc(ada_mm[dc], 1)

            def ada_turn(r, dc):
                pe.wait_ge(ada_rows[dc], r + 1)
                before(ada_taken, r, dc)
                bank = (ps_turn, ps_prep[0])[dc % 2]
                for i in range(RG):
                    last = nc_mm(bank[:, i * NG * B:(i + 1) * NG * B], ada_row[dc % 2][:, i * P:i * P + P], pick[:],
                                 start=True, stop=True)
                last.then_inc(ada_turned[dc], 1)

            def ada_matrix(r):
                ada_products(r, 0)
                for dc in range(1, KC):
                    ada_products(r, dc)
                    ada_turn(r, dc - 1)
                ada_turn(r, KC - 1)

            def turn_rows(q, bank, rounds):
                for dc in range(KC):
                    pe.wait_ge(ada_taken[dc], rounds)
                for c in range(KC):
                    last = turn(bank[0:BR, c * P:c * P + P], ada[:, q, c, :], ident[:])
                last.then_inc(rows_turned, 1)

            def low_rank_matmul(i, bank, weights, rhs, rank_weights, rank_rhs, rank_taken, together=False):
                l, c = divmod(i, KC + 1)
                dst, cols = bank[:, l * TOK:l * TOK + TOK], slice(l * P, l * P + P)
                if c < KC:
                    return nc_mm(dst, weights[:, c, cols], rhs[:, c], start=(c == 0 and not (together and l)), stop=False)
                if l == 0:
                    pe.wait_ge(prep_taken, rank_taken)
                return nc_mm(dst, rank_weights[:, cols], rank_rhs, start=False,
                             stop=(l == KC - 1 or not together))

            def prep(m16, k, par, banks=rank_x1_banks):
                ps_rank, ps_x1 = banks
                for unit, i in SLOT[k]:
                    if unit == "u":
                        if i == 0:
                            pe.wait_ge(x_turned, m16 + 16)
                        last = nc_mm(ps_rank[0:BR, 0:TOK], ada[:, 2, i], x_t[:, i], start=(i == 0), stop=(i == KC - 1))
                    elif unit == "mid":
                        last = low_rank_matmul(i, ps_mid, down_sb, x_t, b2_t, u_m, m16 + TAKEN["u"])
                    elif unit == "v":
                        if i == 0:
                            pe.wait_ge(prep_taken, m16 + TAKEN["mid"])
                        last = nc_mm(ps_rank[0:BR, 0:TOK], ada[:, 1, i], mid_t[:, i], start=(i == 0), stop=(i == KC - 1))
                    elif unit == "x1":
                        last = low_rank_matmul(i, ps_x1, up_t, mid_t, a1_t, v_m, m16 + TAKEN["v"])
                    else:
                        piece = int(unit[2:])
                        nh, g = divmod(piece, GATES)
                        if i == 0:
                            pe.wait_ge(prep_taken, m16 + TAKEN[f"wx{piece - 2}" if piece > 1 else "x1"])
                        h, c = divmod(i, KC)
                        col = g * D + (HC * nh + h) * P
                        last = nc_mm(ps_prep[piece % 2][:, h * TOK:h * TOK + TOK], wx_sb[:, c, col:col + P],
                                     x1_t[par][:, c], start=(c == 0), stop=(c == KC - 1))
                last.then_inc(prep_mm, 1)

            def keep_warm():
                for _ in range(WARM):
                    nc_mm(ps_mid[:, 0:P], ident[:], ident[:], start=True, stop=True)

            def recur(t):
                def products(c, nh):
                    for w in range(PARTS):
                        rhs = wh_parts[:, w, c].rearrange("p (g c) -> p g c", g=GATES)
                        for j in range(NG):
                            u0 = P * j + HU * nh
                            last = nc_mm(ps_rec[nh][GROUP * j:GROUP * j + GROUP, 0:GATES * HU],
                                         h_bits[:, c, :, 1], rhs[:, :, u0:u0 + HU],
                                         start=(c == 0 and w == 0), stop=(c == KC - 1 and w == PARTS - 1),
                                         tile_position=(0, GROUP * j))
                    return last

                pe.wait_ge(h_ready[0], t + 1)
                products(0, 0)
                products(1, 0)
                products(0, 1)
                pe.wait_ge(h_ready[1], t + 1)
                products(2, 0)
                products(3, 0).then_inc(rec_mm[0], 1)
                for c in range(1, KC - 1):
                    products(c, 1)
                products(KC - 1, 1).then_inc(rec_mm[1], 1)

            def step(t, s, par, prepare):
                recur(t)
                if prepare:
                    prep(t - s + BT, s, 1 - par)
                elif s < BT - 1:
                    keep_warm()

            pe.wait_ge(hid_ready, KC)
            ada_matrix(0)
            ada_matrix(1)
            pe.wait_ge(up_ready, KC)
            turn_rows(2, ps_rec[0], 1)
            turn_rows(3, ps_prep[1], 2)
            pe.wait_ge(rows_ready, 1)
            for c in range(KC):
                last = turn(ps_rec[1][:, c * BR:c * BR + BR], a2_t[:, c * P:c * P + P], ident[0:BR, 0:BR])
            last.then_inc(a2_turned, 1)
            pe.wait_ge(a2_ready, 1)
            pe.wait_ge(rows_ready, 2)
            pe.wait_ge(down_loaded, 16 * KC)
            for k in range(MID_SLOT + 1):
                prep(0, k, 0, first_banks)
            pe.wait_ge(prep_taken, TAKEN["mid"])
            x1_args = first_banks[1], up_t, mid_t, a1_t, v_m, TAKEN["v"], True
            for l in range(KC):
                for c in range(KC):
                    low_rank_matmul(l * (KC + 1) + c, *x1_args)
            with pe.Fori(2, 4) as r:
                ada_matrix(r)
            turn_rows(0, ps_prep[1], 4)
            for c in range(KC):
                last = nc_mm(first_banks[0][0:BR, 0:TOK], ada[:, 1, c], mid_t[:, c], start=(c == 0), stop=(c == KC - 1))
            last.then_inc(prep_mm, V_SLOT - MID_SLOT)
            pe.wait_ge(rows_ready, 3)
            for l in range(KC):
                last = low_rank_matmul(l * (KC + 1) + KC, *x1_args)
            last.then_inc(prep_mm, X1_SLOT - V_SLOT)
            pe.wait_ge(wx_folded, GATES * KC)
            for k in range(X1_SLOT + 1, BT):
                prep(0, k, 0)
            pe.wait_ge(wh_split, KC)
            for s in range(BT):
                step(s, s, 0, True)
            with pe.Fori(BT, T - BT, 2 * BT) as t0:
                for s in range(2 * BT):
                    step(t0 + s, s % BT, 1 - s // BT, True)
            for s in range(BT):
                step(T - BT + s, s, 1, False)

        @block.vector
        def _(dve):
            stt = nc.vector.scalar_tensor_tensor
            tt = nc.vector.tensor_tensor
            ts = nc.vector.tensor_scalar
            nc.vector.memset(h_sb[:], 0.0).then_inc(cleared, 1)
            nc.vector.memset(hid_t[:], 0.0).then_inc(cleared, 1)
            for nh in pair:
                nc.vector.memset(gates[nh][:], 0.0).then_inc(cleared, 1)

            dve.wait_ge(cond_loaded, 16)
            nc.vector.tensor_copy(by_fold(cond_f), folded(cond_sb[:])).then_inc(cond_folded, 1)
            nc.vector.reduce_sum(stat[:, 0:1], cond_sb[:], AX.X).then_inc(ln_step, 1)
            dve.wait_ge(ln_step, 1)
            ts(stat[:, 0:1], stat[:, 0:1], 1.0 / D, None, ALU.mult).then_inc(ln_step, 1)
            dve.wait_ge(ln_step, 2)
            ts(cond_n, cond_sb[:], stat[:, 0:1], None, ALU.subtract).then_inc(ln_step, 1)
            dve.wait_ge(ln_step, 3)
            tt(cond_sb[:], cond_n, cond_n, ALU.mult).then_inc(ln_step, 1)
            dve.wait_ge(ln_step, 4)
            nc.vector.reduce_sum(stat[:, 1:2], cond_sb[:], AX.X).then_inc(ln_step, 1)
            dve.wait_ge(ln_step, 5)
            ts(stat[:, 2:3], stat[:, 1:2], 1.0 / D, LN_EPS, ALU.mult, ALU.add).then_inc(ln_var, 1)
            dve.wait_ge(ln_var, 1)
            dve.wait_ge(ln_root, 1)
            nc.vector.reciprocal(stat[:, 4:5], stat[:, 3:4]).then_inc(ln_step, 1)
            dve.wait_ge(ln_step, 6)
            stt(stat[:, 5:6], stat[:, 2:3], stat[:, 4:5], stat[:, 3:4], ALU.mult, ALU.add).then_inc(ln_step, 1)
            dve.wait_ge(ln_step, 7)
            ts(stat[:, 6:7], stat[:, 5:6], 0.5, None, ALU.mult).then_inc(ln_step, 1)
            dve.wait_ge(ln_step, 8)
            nc.vector.reciprocal(stat[:, 7:8], stat[:, 6:7]).then_inc(ln_step, 1)
            dve.wait_ge(ln_step, 9)
            ts(cond_n, cond_n, stat[:, 7:8], None, ALU.mult).then_inc(ln_done, 1)

            dve.wait_ge(vecs_turned, 1)
            nc.vector.tensor_copy(vecs_t[:], ps_prep[1][:, 0:VECS]).then_inc(vecs_ready, 1)
            dve.wait_ge(vecs_ready, 1)
            dve.wait_ge(cond_turned, 1)
            for c in range(KC):
                ts(cond_t[:, c], ps_ada[0][:, c * B:c * B + B], gamma_t[:, c:c + 1], beta_t[:, c:c + 1],
                   ALU.mult, ALU.add).then_inc(cond_ready, 1)

            dve.wait_ge(cleared, 4)
            dve.wait_ge(state_turned, 1)
            for nh in pair:
                ts(h2[nh], by_chunk(ps_ada[1][:, nh * HG:nh * HG + HG]), 2.0, None, ALU.mult).then_inc(h_full[nh], 1)
                dve.wait_ge(h_full[nh], 1)
                tt(rest1[nh], h2[nh], h2_hi[nh], ALU.subtract).then_inc(h_rest[nh], 1)
                dve.wait_ge(h_rest[nh], 1)
                tt(rest2[nh], rest1[nh], rest1_hi[nh], ALU.subtract).then_inc(h_ready[nh], 1)

            for l in range(KC):
                dve.wait_ge(up_turned, l + 1)
                nc.vector.tensor_copy(by_fold(up_t[:, l]), folded((ps_prep[1], ps_mid)[l % 2][:])).then_inc(up_ready, 1)

            ts(gate_bias[:, :, GATES - 1], gate_bias[:, :, GATES - 1], 2.0, None, ALU.mult).then_inc(bias_doubled, 1)
            dve.wait_ge(bias_doubled, 1)

            dve.wait_ge(consts_loaded, 16 * 4)

            def ada_copy(r, dc):
                dve.wait_ge(ada_mm[dc], r + 1)
                if dc >= 2:
                    dve.wait_ge(ada_turned[dc - 2], r + 1)
                elif not (isinstance(r, int) and r == 0):
                    dve.wait_ge(ada_turned[dc + 2], r)
                nc.vector.tensor_copy(ada_row[dc % 2][:], ps_ada[dc % 2][:, 0:RG * P]).then_inc(ada_rows[dc], 1)

            def ada_store(r, q, dc):
                dve.wait_ge(ada_turned[dc], r + 1)
                src = (ps_turn, ps_prep[0])[dc % 2][:, 0:BR].rearrange("p (r g b) -> p r g b", r=RG, b=B)
                dst = ada[:, bass.ds(q, 1), dc].rearrange("p q (g r b) -> p (q r) g b", g=NG, b=B)
                bias = bias2_sb[:, bass.ds(q, 1), dc].rearrange("p q (g r) -> p (q r) g", g=NG)
                tt(dst, src, bias.unsqueeze(3).broadcast_to([P, RG, NG, B]), ALU.add).then_inc(ada_taken[dc], 1)

            def ada_matrix(r, q):
                ada_copy(r, 0)
                for dc in range(1, KC):
                    ada_copy(r, dc)
                    ada_store(r, q, dc - 1)
                ada_store(r, q, KC - 1)

            def turn_x(m16):
                dve.wait_ge(x_loaded, NDMA * (m16 + 16))
                nc.vector.transpose(x_t, blocks_of_32(x_sb[:])).then_inc(x_turned, 16)

            def turn_y(t0, par, first=False):
                dve.wait_ge(y_added, t0 + 16)
                if not first:
                    dve.wait_ge(y_stored, NDMA * t0)
                nc.vector.transpose(blocks_of_32(y_sb), y_t[par]).then_inc(y_turned, 16)

            def prep(m16, k, par, banks=rank_x1_banks):
                ps_rank, ps_x1 = banks
                for unit in FINISHED[k]:
                    if unit == "mid":
                        continue
                    dve.wait_ge(prep_mm, m16 + k + 1)
                    if unit in ("u", "v"):
                        last = tt(u_m if unit == "u" else v_m, ps_rank[0:BR, 0:TOK], mask[:], ALU.mult)
                    elif unit == "x1":
                        dve.wait_ge(x_turned, m16 + 16)
                        last = stt(x1_t[par].rearrange("p c t -> p (c t)"), x_t.rearrange("p c t -> p (c t)"), 2.0,
                                   ps_x1[:], ALU.mult, ALU.add)
                    else:
                        piece = int(unit[2:])
                        nh, g = divmod(piece, GATES)
                        dst = xw[par][:, :, nh, g * HG:g * HG + HG].rearrange("p t (c b) -> p c t b", b=B)
                        src = ps_prep[piece % 2][:, 0:HC * TOK].rearrange("p (c t b) -> p c t b", c=HC, b=B)
                        bias = gate_bias[:, nh, g].unsqueeze(2).unsqueeze(3).broadcast_to([P, HC, BT, B])
                        last = tt(dst, src, bias, ALU.add)
                    last.then_inc(prep_taken, BT + 1 - len(UNITS) if unit == UNITS[-1][0] else 1)

            def turn_half(t, nh):
                dve.wait_ge(rec_mm[nh], t + 1)
                nc.vector.transpose(turned[nh], ps_rec[nh][:, 0:GATES * HU]).then_inc(turn_done[nh], 1)

            def sum_parts(t, nh):
                dve.wait_ge(turn_done[nh], t + 1)
                src = turned[nh].rearrange("p (g q b) -> p g b q", b=B, q=GROUP // B)[:, :, :, 0:PARTS]
                nc.vector.tensor_reduce(summed[nh][:].rearrange("p (g b) -> p g b", b=B), src, AX.X,
                                        ALU.add).then_inc(sum_done[nh], 1)

            def add_projection(t, s, par, nh):
                dve.wait_ge(sum_done[nh], t + 1)
                tt(inputs[nh][:], summed[nh][:], xw[par][:, s, nh], ALU.add).then_inc(inputs_done[nh], 1)

            def products(t, nh):
                dve.wait_ge(gates_done[nh], t + 1)
                g = gates[nh]
                stt(prods[nh][:], g[:, 0:2 * HG], 1.0, g[:, 3 * HG:5 * HG], ALU.add, ALU.mult).then_inc(prods_done[nh], 1)

            def cell(t, nh):
                dve.wait_ge(prods_done[nh], t + 1)
                stt(gates[nh][:, 4 * HG:], prods[nh][:, HG:], 0.5, prods[nh][:, 0:HG], ALU.mult, ALU.add).then_inc(c_done[nh], 1)

            def hidden(t, nh):
                dve.wait_ge(tanh_c_done[nh], t + 1)
                stt(h2[nh], by_chunk(gates[nh][:, 2 * HG:3 * HG]), 1.0, by_chunk(tanh_c[nh][:]),
                    ALU.add, ALU.mult).then_inc(h_full[nh], 1)

            def remainder1(t, nh):
                dve.wait_ge(h_full[nh], t + 2)
                tt(rest1[nh], h2[nh], h2_hi[nh], ALU.subtract).then_inc(h_rest[nh], 1)

            def remainder2(t, nh):
                dve.wait_ge(h_rest[nh], t + 2)
                tt(rest2[nh], rest1[nh], rest1_hi[nh], ALU.subtract).then_inc(h_ready[nh], 1)

            def step(t, s, par, prepare, output):
                if s == 0 and prepare:
                    turn_x(t + BT)
                turn_half(t, 0)
                sum_parts(t, 0)
                add_projection(t, s, par, 0)
                products(t, 0)
                turn_half(t, 1)
                cell(t, 0)
                sum_parts(t, 1)
                hidden(t, 0)
                add_projection(t, s, par, 1)
                remainder1(t, 0)
                remainder2(t, 0)
                products(t, 1)
                cell(t, 1)
                hidden(t, 1)
                remainder1(t, 1)
                remainder2(t, 1)
                stt(y_t[par][:, :, s * B:s * B + B], h_sb[:, :, 0:B], 0.5, x1_t[par][:, :, s * B:s * B + B],
                    ALU.mult, ALU.add).then_inc(y_added, 1)
                if s == Y_STEP and output:
                    turn_y(t - s - BT, 1 - par)
                if prepare:
                    prep(t - s + BT, s, 1 - par)

            ada_matrix(0, 2)
            ada_matrix(1, 3)
            dve.wait_ge(rows_turned, 1)
            nc.vector.tensor_copy(by_fold(a2_t), folded(ps_rec[0][0:BR, :])).then_inc(rows_ready, 1)
            dve.wait_ge(rows_turned, 2)
            nc.vector.tensor_copy(b2_t[:], ps_prep[1][0:BR, :]).then_inc(rows_ready, 1)
            turn_x(0)
            dve.wait_ge(a2_turned, 1)
            nc.vector.tensor_copy(ada[:, 2].rearrange("p c r -> p (c r)"), ps_rec[1][:, 0:KC * BR]).then_inc(a2_ready, 1)
            for k in range(MID_SLOT + 1):
                prep(0, k, 0, first_banks)
            with dve.Fori(0, 2) as q:
                ada_matrix(q + 2, q)
            dve.wait_ge(rows_turned, 3)
            nc.vector.tensor_copy(by_fold(a1_t[:]), folded(ps_prep[1][0:BR, :])).then_inc(rows_ready, 1)
            for k in range(MID_SLOT + 1, BT):
                prep(0, k, 0, first_banks)
            dve.wait_ge(prep_taken, BT)
            for s in range(BT):
                step(s, s, 0, True, False)
            with dve.Fori(BT, T - BT, 2 * BT) as t0:
                for s in range(2 * BT):
                    if s % BT == 0:
                        dve.wait_ge(prep_taken, t0 + s + BT)
                    step(t0 + s, s % BT, 1 - s // BT, True, True)
            dve.wait_ge(prep_taken, T)
            for s in range(BT):
                step(T - BT + s, s, 1, False, True)
            turn_y(T - BT, 1)


_INS = ['x', 'cond_1024', 'L0_cond_base_up', 'L0_cond_base_down', 'L0_cond_ln_gamma', 'L0_cond_ln_beta',
        'L0_cond_W1', 'L0_cond_bias1', 'L0_cond_W2', 'L0_cond_bias2', 'L1_cond_Wx', 'L1_cond_Wh', 'L1_cond_b']


def shape_constants(B, R):
    import numpy as np

    ident = np.eye(P, dtype=np.float32)
    pick = np.zeros((P, NG * B), np.float32)
    for g in range(NG):
        for b in range(B):
            pick[GROUP * g + b, g * B + b] = 1
    mask = (np.arange(B * R)[:, None] % B == np.arange(P)[None, :] % B).astype(np.float32)
    return {"ident": ident, "pick": pick, "mask": mask}


def kernel(**inputs):
    import numpy as _np
    import concourse.bacc as _bacc
    from concourse import mybir as _mybir
    from concourse.bass_utils import run_bass_kernel_spmd as _run

    nc = _bacc.Bacc("TRN2", target_bir_lowering=False, num_devices=1)
    arrays = {f"in_{name}_dram": _np.ascontiguousarray(inputs[name]) for name in _INS}
    B, T, D = inputs['x'].shape
    for name, a in shape_constants(B, inputs['L0_cond_W2'].shape[1] // (4 * D)).items():
        arrays[f"const_{name}_dram"] = a
    args = [nc.dram_tensor(n, a.shape, _mybir.dt.from_np(a.dtype), kind="ExternalInput").ap() for n, a in arrays.items()]
    args.append(nc.dram_tensor("out_0_dram", (B, T, D), _mybir.dt.float32, kind="ExternalOutput").ap())
    cond_residual_lstm(nc, *args)
    r = _run(nc, [arrays], core_ids=[0])
    return r.results[0]["out_0_dram"]
```
